# Optimizing a Trainium2 kernel written in Bass

```python
import numpy as np
import jax
import jax.numpy as jnp

def _softmax(x, axis=-1):
    return jax.nn.softmax(x, axis=axis)

def _gelu(x):
    return jax.nn.gelu(x, approximate=True)

def _silu(x):
    return jax.nn.silu(x)

def _sigmoid(x):
    return jax.nn.sigmoid(x)

def _layernorm(x, axis=-1, eps=1e-05):
    m = jnp.mean(x, axis=axis, keepdims=True)
    v = jnp.var(x, axis=axis, keepdims=True)
    return (x - m) / jnp.sqrt(v + eps)

def _scatter_add(tgt, idx, src, axis=0):
    return tgt.at[idx].add(src)

def _segment_sum(src, seg, n):
    return jax.ops.segment_sum(src, seg, n)
kernel_name = 'mk_conv_preact_d2_conv_nchw256_r2_c98a7c'

def setup_inputs(seed: int=0):
    np.random.seed(seed)
    _w = jnp.asarray

    def _rec_inputs():
        import jax
        import jax.numpy as jnp
        _gk = jax.random.key(seed)
        x = -0.000125 + 0.9999 * jax.random.normal(jax.random.fold_in(_gk, 1), (32, 128, 32, 32), jnp.float32)
        return x
    x = _rec_inputs()

    def _L0_conv_setup():
        import jax, jax.numpy as jnp
        from jax import lax
        import numpy as np
        DATA_CHANNELS = 3
        CIN = 128
        S = 128
        B, H, W = (32, 32, 32)
        DN = ('NCHW', 'OIHW', 'NCHW')

        def build_mask_B(out_c, in_c, dc):
            m = np.zeros((out_c, in_c, 1, 3), dtype=np.float32)
            m[:, :, 0, :2] = 1.0
            oc = np.arange(out_c) % dc
            ic = np.arange(in_c) % dc
            bad = oc[:, None] < ic[None, :]
            center = m[:, :, 0, 1]
            center[bad] = 0.0
            m[:, :, 0, 1] = center
            return jnp.asarray(m)
        key = jax.random.key(seed)
        ks = jax.random.split(key, 8)
        sc = 0.05
        return {'x': jax.random.normal(ks[0], (B, CIN, H, W), dtype=jnp.float32), 'w_i2s': jax.random.normal(ks[1], (S, CIN, 1, 3), dtype=jnp.float32) * sc, 'b_i2s': jax.random.normal(ks[2], (S,), dtype=jnp.float32) * sc, 'w_s2s': jax.random.normal(ks[3], (S, S, 1, 3), dtype=jnp.float32) * sc, 'b_s2s': jax.random.normal(ks[4], (S,), dtype=jnp.float32) * sc, 'w_ih': jax.random.normal(ks[5], (4 * S, S), dtype=jnp.float32) * sc, 'b_ih': jax.random.normal(ks[6], (4 * S,), dtype=jnp.float32) * sc, 'b_hh': jax.random.normal(ks[7], (4 * S,), dtype=jnp.float32) * sc}
    _L0_conv_all = _L0_conv_setup()
    _L0_conv_in = {k: v for k, v in _L0_conv_all.items() if k in ('w_i2s', 'b_i2s', 'w_s2s', 'b_s2s', 'w_ih', 'b_ih', 'b_hh')}
    del _L0_conv_all

    def _L1_conv_setup():
        import jax, jax.numpy as jnp
        from jax import lax
        import numpy as np

        def _het_mask(out_f, in_f, p):
            n = jnp.arange(out_f)[:, None]
            i = jnp.arange(in_f)[None, :]
            is3x3 = (i - n) % p == 0
            center = jnp.zeros((3, 3), jnp.float32).at[1, 1].set(1.0)
            full = jnp.ones((3, 3), jnp.float32)
            return jnp.where(is3x3[:, :, None, None], full, center)
        key = jax.random.key(seed)
        k1, k2, k3 = jax.random.split(key, 3)
        B, C_in, C_out, H, W_sp = (32, 128, 128, 56, 56)
        x = jax.random.normal(k1, (B, C_in, H, W_sp), dtype=jnp.float32)
        fan_in = 9.0
        W = jax.random.normal(k2, (C_out, C_in, 3, 3), dtype=jnp.float32) * (1.0 / np.sqrt(fan_in))
        b = jax.random.normal(k3, (C_out, C_in), dtype=jnp.float32) * 0.05
        return {'x': x, 'W': W, 'b': b, 'p': 4}
    _L1_conv_all = _L1_conv_setup()
    _L1_conv_in = {k: v for k, v in _L1_conv_all.items() if k in ('W', 'b')}
    del _L1_conv_all
    return {'x': x, 'L0_conv_w_i2s': _L0_conv_in['w_i2s'], 'L0_conv_b_i2s': _L0_conv_in['b_i2s'], 'L0_conv_w_s2s': _L0_conv_in['w_s2s'], 'L0_conv_b_s2s': _L0_conv_in['b_s2s'], 'L0_conv_w_ih': _L0_conv_in['w_ih'], 'L0_conv_b_ih': _L0_conv_in['b_ih'], 'L0_conv_b_hh': _L0_conv_in['b_hh'], 'L1_conv_W': _L1_conv_in['W'], 'L1_conv_b': _L1_conv_in['b']}

def reference(x, L0_conv_w_i2s, L0_conv_b_i2s, L0_conv_w_s2s, L0_conv_b_s2s, L0_conv_w_ih, L0_conv_b_ih, L0_conv_b_hh, L1_conv_W, L1_conv_b):
    import jax
    import jax.numpy as jnp

    def _L0_conv_ref(x, w_i2s, b_i2s, w_s2s, b_s2s, w_ih, b_ih, b_hh):
        import jax, jax.numpy as jnp
        from jax import lax
        import numpy as np
        DATA_CHANNELS = 3
        CIN = 128
        S = 128
        B, H, W = (32, 32, 32)
        DN = ('NCHW', 'OIHW', 'NCHW')

        def build_mask_B(out_c, in_c, dc):
            m = np.zeros((out_c, in_c, 1, 3), dtype=np.float32)
            m[:, :, 0, :2] = 1.0
            oc = np.arange(out_c) % dc
            ic = np.arange(in_c) % dc
            bad = oc[:, None] < ic[None, :]
            center = m[:, :, 0, 1]
            center[bad] = 0.0
            m[:, :, 0, 1] = center
            return jnp.asarray(m)
        b, cin, h_dim, w_dim = x.shape
        s = w_i2s.shape[0]
        mask = build_mask_B(s, cin, DATA_CHANNELS)
        xs = lax.conv_general_dilated(x, w_i2s * mask, (1, 1), [(0, 0), (1, 1)], dimension_numbers=DN) + b_i2s[None, :, None, None]
        x_rows = jnp.transpose(xs, (2, 0, 3, 1)).reshape(h_dim, b * w_dim, s)
        bias = b_ih + b_hh

        def step(carry, x_row):
            h, c = carry
            hc = lax.conv_general_dilated(h.T[None, :, None, :], w_s2s, (1, 1), [(0, 0), (1, 1)], dimension_numbers=DN)
            hc = hc[0, :, 0, :].T + b_s2s
            gates = (x_row + hc) @ w_ih.T + bias
            i, f, g, o = jnp.split(gates, 4, axis=-1)
            c = jax.nn.sigmoid(f) * c + jax.nn.sigmoid(i) * jnp.tanh(g)
            h = jax.nn.sigmoid(o) * jnp.tanh(c)
            return ((h, c), h)
        init = (jnp.zeros((b * w_dim, s), x.dtype), jnp.zeros((b * w_dim, s), x.dtype))
        _, hs = lax.scan(step, init, x_rows)
        out = hs.reshape(h_dim, b, s, w_dim)
        return jnp.transpose(out, (1, 2, 0, 3))

    def _L1_conv_ref(x, W, b, p):
        import jax, jax.numpy as jnp
        from jax import lax
        import numpy as np

        def _het_mask(out_f, in_f, p):
            n = jnp.arange(out_f)[:, None]
            i = jnp.arange(in_f)[None, :]
            is3x3 = (i - n) % p == 0
            center = jnp.zeros((3, 3), jnp.float32).at[1, 1].set(1.0)
            full = jnp.ones((3, 3), jnp.float32)
            return jnp.where(is3x3[:, :, None, None], full, center)
        out_f, in_f = (W.shape[0], W.shape[1])
        Wm = W * _het_mask(out_f, in_f, p)
        y = lax.conv_general_dilated(x, Wm, window_strides=(1, 1), padding=((1, 1), (1, 1)), dimension_numbers=('NCHW', 'OIHW', 'NCHW'))
        return y + jnp.sum(b, axis=1)[None, :, None, None]

    def _gn(v, G=32, eps=1e-05):
        B_, C_, H_, W_ = v.shape
        g = v.reshape(B_, G, C_ // G, H_, W_)
        m = jnp.mean(g, axis=(2, 3, 4), keepdims=True)
        s = jnp.var(g, axis=(2, 3, 4), keepdims=True)
        return ((g - m) / jnp.sqrt(s + eps)).reshape(v.shape)

    def _ln_c(v, eps=1e-06):
        m = jnp.mean(v, axis=1, keepdims=True)
        s = jnp.var(v, axis=1, keepdims=True)
        return (v - m) / jnp.sqrt(s + eps)

    def _ln_t(v, eps=1e-05):
        m = jnp.mean(v, axis=-1, keepdims=True)
        s = jnp.var(v, axis=-1, keepdims=True)
        return (v - m) / jnp.sqrt(s + eps)

    def _to_tokens(v):
        B_, C_, H_, W_ = v.shape
        return v.reshape(B_, C_, H_ * W_).transpose(0, 2, 1)

    def _from_tokens(t, like):
        B_, C_, H_, W_ = like.shape
        return t.transpose(0, 2, 1).reshape(B_, C_, H_, W_)
    x = x + _L0_conv_ref(_gn(x), L0_conv_w_i2s, L0_conv_b_i2s, L0_conv_w_s2s, L0_conv_b_s2s, L0_conv_w_ih, L0_conv_b_ih, L0_conv_b_hh)
    x = x + _L1_conv_ref(_gn(x), L1_conv_W, L1_conv_b, 4)
    return x

_drawn_inputs = setup_inputs


def setup_inputs(seed=0):
    import zlib

    import numpy as np

    out = dict(_drawn_inputs(seed))
    spreads = {}
    factors = {'L0_conv_b_i2s': 4.902,
     'L0_conv_w_s2s': 2.754,
     'L0_conv_b_s2s': 4.623,
     'L0_conv_b_ih': 3.037,
     'L0_conv_b_hh': 2.93}
    for name, (base, spread) in spreads.items():
        noise = np.random.default_rng([zlib.crc32(name.encode()), seed]).standard_normal(out[name].shape)
        drawn = base * np.exp(spread * noise) if base else spread * noise
        out[name] = jnp.asarray(drawn.astype(out[name].dtype))
    for name, factor in factors.items():
        out[name] = (out[name] * factor).astype(out[name].dtype)
    return out
```

```python
from contextlib import ExitStack

import numpy as np
import concourse.bass as bass
from concourse import mybir

F32 = mybir.dt.float32
F32R = mybir.dt.float32r
F16 = mybir.dt.float16
I32 = mybir.dt.int32
ALU = mybir.AluOpType
ACT = mybir.ActivationFunctionType
AX = mybir.AxisListType

P = 128
B, H, W = 32, 32, 32
HW = H * W
Q = 4
GATES = 4

ACT_SCALE = 512.0
WEIGHT_TOP = 4096.0
EXPONENT_BITS = 0x7F800000

BLOCKS = [(0, 11), (11, 21), (21, 32)]
NB = len(BLOCKS)
ITEMS = NB * H
F_GATE, I_GATE, G_GATE, O_GATE = 1, 0, 2, 3
GATE_ORDER = [F_GATE, I_GATE, G_GATE, O_GATE]
GATE_BANKS = 6

CH = 4
CHUNKS = B // CH
GN_STEPS = 10

H_AHEAD = 2
Z_AHEAD = 1
ROW_AHEAD = 2
STORE_LAG = 6


def width(k):
    return W * (BLOCKS[k][1] - BLOCKS[k][0])


PADW = W + 1
PADN = 1 + (H + 2) * PADW + 1


def build_network(nc, x, w_i2s, b_i2s, w_s2s, b_s2s, w_ih, b_ih, b_hh, w_conv, b_conv, consts, out):
    x_q = x.rearrange("b (n q) h w -> q n b (h w)", q=Q)
    out_q = out.rearrange("b (n q) h w -> q b n (h w)", q=Q)

    with ExitStack() as ctx:
        def sb(name, shape, dt, stack=ctx):
            return stack.enter_context(nc.sbuf_tensor(name, shape, dt))

        def sem(name):
            return ctx.enter_context(nc.semaphore(name))

        img = sb("img", [P, B, H, 2, W], F16)
        img32 = img[:].rearrange("p b h s w -> p (b h s w)").bitcast(F32).rearrange("p (b h w) -> p b h w", b=B, h=H)
        ident = sb("ident", [P, P], F32)
        group_mean = sb("group_mean", [P, P], F32)
        wi_hi = sb("wi_hi", [P, 2, P], F16)
        wi_lo = sb("wi_lo", [P, 2, P], F16)
        ws_hi = sb("ws_hi", [P, 3, P], F16)
        ws_lo = sb("ws_lo", [P, 3, P], F16)
        wg_hi = sb("wg_hi", [P, GATES, P], F32R)
        wg_lo = sb("wg_lo", [P, GATES, P], F32R)
        wc_hi = sb("wc_hi", [P, 9, P], F16)
        wc_lo = sb("wc_lo", [P, 9, P], F16)
        z_unscale = sb("z_unscale", [P, 1], F32)
        y_unscale = sb("y_unscale", [P, 1], F32)
        gate_bias = sb("gate_bias", [P, GATES], F32)
        conv_bias = sb("conv_bias", [P, 1], F32)
        bn = sb("bn", [P, CH, 2, 6], F32)
        mv = sb("mv", [P, CH, 2], F32)
        gmean = sb("gmean", [P, CH], F32)
        dev = sb("dev", [P, CH], F32)
        dev2 = sb("dev2", [P, CH], F32)
        vdev = sb("vdev", [P, CH], F32)
        var_eps = sb("var_eps", [P, CH], F32)
        sd = sb("sd", [P, CH], F32)
        rs0 = sb("rs0", [P, CH], F32)
        nt = [sb(f"nt{i}", [P, CH], F32) for i in range(3)]
        rstd = sb("rstd", [P, CH], F32)

        with ExitStack() as s0:
            stage = [sb(f"stage{i}", [P, CH, HW], F32, s0) for i in range(2)]
            raw_i = sb("raw_i", [P, P, 3], F32, s0)
            raw_s = sb("raw_s", [P, P, 3], F32, s0)
            raw_g = sb("raw_g", [P, GATES, P], F32, s0)
            raw_c = sb("raw_c", [P, P, 9], F32, s0)
            turn_i = sb("turn_i", [P, 2, P], F32, s0)
            turn_c = sb("turn_c", [P, 9, P], F32, s0)
            raw_cb = sb("raw_cb", [P, P], F32, s0)
            mask = sb("mask", [P, P], F32, s0)
            wgT = sb("wgT", [P, GATES, P], F32, s0)
            brow = sb("brow", [P, 2 + 2 * GATES], F32, s0)
            bsum = sb("bsum", [P, 1 + GATES], F32, s0)
            top = sb("top", [P, 8], F32, s0)
            scl = sb("scl", [P, 6], F32, s0)
        with ExitStack() as s1:
            cell = sb("cell", [P, B * W], F32, s1)
            hrow = [sb(f"hrow{i}", [P, B * W], F32, s1) for i in range(2)]
            hh = [sb(f"hh{i}", [P, B * W + 2], F16, s1) for i in range(2)]
            hl = [sb(f"hl{i}", [P, B * W + 2], F16, s1) for i in range(2)]
            gate = [[sb(f"gate{i}{j}", [P, 352], F32, s1) for j in range(GATES)] for i in range(2)]
            fc = [sb(f"fc{i}", [P, 352], F32, s1) for i in range(2)]
            ig = [sb(f"ig{i}", [P, 352], F32, s1) for i in range(2)]
            hT = [sb(f"hT{i}", [P, 352], F32, s1) for i in range(2)]
            tc = [sb(f"tc{i}", [P, 352], F32, s1) for i in range(2)]
            z_hi = sb("z_hi", [P, 352], F32R, s1)
            z_lo = sb("z_lo", [P, 352], F32R, s1)
        with ExitStack() as s2:
            xs = [sb(f"xs{i}", [P, HW], F32, s2) for i in range(2)]
            xn = [sb(f"xn{i}", [P, HW], F32, s2) for i in range(2)]
            pad_hi = [sb(f"pad_hi{i}", [P, PADN], F16, s2) for i in range(2)]
            pad_lo = [sb(f"pad_lo{i}", [P, PADN], F16, s2) for i in range(2)]
            ybuf = [sb(f"ybuf{i}", [P, HW], F32, s2) for i in range(2)]

        ps = ctx.enter_context(nc.psum_tensor("ps", [P, 8, 512], F32))

        par_in = sem("par_in")
        x_in = [sem(f"x_in{i}") for i in range(2)]
        prep = sem("prep")
        raws_ready = sem("raws_ready")
        bias_ready = sem("bias_ready")
        prep_T = sem("prep_T")
        wgt_done = sem("wgt_done")
        prep_hi = sem("prep_hi")
        waited = sem("waited")
        bn_done = sem("bn_done")
        aggr_done = sem("aggr_done")
        mean_ready = sem("mean_ready")
        var_ready = sem("var_ready")
        gn_step = sem("gn_step")
        sd_done = sem("sd_done")
        xn0_done = sem("xn0_done")
        hi0_done = sem("hi0_done")
        lo0_done = sem("lo0_done")
        z_ready = sem("z_ready")
        z_hi_done = sem("z_hi_done")
        z_lo_done = sem("z_lo_done")
        gate_ready = sem("gate_ready")
        gate_done = sem("gate_done")
        fc_done = sem("fc_done")
        ig_done = sem("ig_done")
        c_done = sem("c_done")
        tc_done = sem("tc_done")
        h_done = sem("h_done")
        hh_done = sem("hh_done")
        hl_done = sem("hl_done")
        wc_zero = sem("wc_zero")
        ht_done = sem("ht_done")
        row_done = sem("row_done")
        xs_in = [sem(f"xs_in{i}") for i in range(2)]
        x1_done = sem("x1_done")
        pads_zero = sem("pads_zero")
        xn_done = sem("xn_done")
        hi_done = sem("hi_done")
        lo_done = sem("lo_done")
        conv_done = sem("conv_done")
        y_done = sem("y_done")
        sum_done = sem("sum_done")
        stored = [sem(f"stored{i}") for i in range(2)]

        block = ctx.enter_context(nc.Block())

        def zbank(it):
            return ps[:, it % 2, :]

        def gbank(it, n):
            return ps[:, 2 + (GATES * it + n) % GATE_BANKS, :]

        gn_ps = ps[:, 7, 0:2 * CH]

        def padded(t, half, dh, dw):
            at = 1 + (16 * half + 1 + dh) * PADW + dw
            return t[:, at:at + 16 * PADW].rearrange("p (h w) -> p h w", w=PADW)[:, :, 0:W]

        def interior(t):
            return t[:, 1 + PADW:1 + PADW + H * PADW].rearrange("p (h w) -> p h w", w=PADW)[:, :, 0:W]

        def wgroup(n):
            return ps[:, n, 0:[2, 3, 4, 3, 3, 3][n] * P].rearrange("p (a b) -> p a b", b=P)

        wconv_ps = ps[:, 3:6, 0:3 * P].rearrange("p d (e o) -> p d e o", o=P)

        def diagonal(t, q):
            return t[32 * q:32 * q + 32, :, :, 32 * q:32 * q + 32]

        def taps33(t):
            return t[:].rearrange("p (d e) o -> p d e o", e=3)

        @block.sync
        def _(sp):
            def load_chunk(g, slot):
                for q in range(Q):
                    sp.dma_start(stage[slot][32 * q:32 * q + 32, :, :],
                                 x_q[q, :, bass.ds(CH * g, CH), :]).then_inc(x_in[slot], 16)

            load_chunk(0, 0)
            sp.dma_start(raw_i[:], w_i2s.rearrange("o i a k -> o i (a k)")).then_inc(par_in, 16)
            sp.dma_start(raw_s[:], w_s2s.rearrange("o i a k -> o i (a k)")).then_inc(par_in, 16)
            sp.dma_start(raw_g[:], w_ih.rearrange("(j p) s -> p j s", p=P)).then_inc(par_in, 16)
            for n, t in enumerate((ident, group_mean, mask)):
                sp.dma_start(t[:], consts[n]).then_inc(par_in, 16)
            with nc.allow_non_contiguous_dma(reason="bias columns"):
                sp.dma_start(brow[:, 0:1], b_i2s.rearrange("(p a) -> p a", a=1)).then_inc(par_in, 16)
                sp.dma_start(brow[:, 1:2], b_s2s.rearrange("(p a) -> p a", a=1)).then_inc(par_in, 16)
                sp.dma_start(brow[:, 2:2 + GATES], b_ih.rearrange("(j p) -> p j", p=P)).then_inc(par_in, 16)
                sp.dma_start(brow[:, 2 + GATES:2 + 2 * GATES], b_hh.rearrange("(j p) -> p j", p=P)).then_inc(par_in, 16)
            for q in range(Q):
                sp.dma_start(raw_c[32 * q:32 * q + 32], w_conv.rearrange("(n q) i a k -> q n i (a k)", q=Q)[q]).then_inc(par_in, 16)
                sp.dma_start(raw_cb[32 * q:32 * q + 32], b_conv.rearrange("(n q) i -> q n i", q=Q)[q]).then_inc(par_in, 16)
            load_chunk(1, 1)
            with sp.Fori(1, CHUNKS // 2) as i:
                for u in range(2):
                    sp.wait_ge(lo0_done, CH * (2 * i + u - 1))
                    load_chunk(2 * i + u, u)

            def load_xs(b, slot):
                for q in range(Q):
                    sp.dma_start(xs[slot][32 * q:32 * q + 32, :], x_q[q, :, b, :]).then_inc(xs_in[slot], 16)

            def store(b, slot):
                sp.wait_ge(sum_done, b + 1)
                for q in range(Q):
                    sp.dma_start(out_q[q, b], ybuf[slot][32 * q:32 * q + 32, :]).then_inc(stored[slot], 16)

            sp.wait_ge(row_done, ROW_AHEAD + ITEMS)
            load_xs(0, 0)
            load_xs(1, 1)
            for b in range(STORE_LAG):
                sp.wait_ge(x1_done, b + 1)
                load_xs(b + 2, b % 2)
            with sp.Fori(STORE_LAG // 2, B // 2 - 1) as i:
                for u in range(2):
                    store(2 * i + u - STORE_LAG, u)
                    sp.wait_ge(x1_done, 2 * i + u + 1)
                    load_xs(2 * i + u + 2, u)
            for b in range(B - 2 - STORE_LAG, B):
                store(b, b % 2)
            for u in range(2):
                sp.wait_ge(stored[u], 16 * Q * (B // 2))

        @block.vector
        def _(v):
            n_prep = [0]

            def step(ins):
                n_prep[0] += 1
                ins.then_inc(prep, 1)

            def settle():
                v.wait_ge(prep, n_prep[0])

            def apart():
                v.sem_inc(waited, 1)

            def bn_stats(src, j):
                for s in range(2):
                    v.bn_stats(bn[:, j, s, :], src[:, 512 * s:512 * s + 512]).then_inc(bn_done, 1)

            def bn_aggr(g):
                v.wait_ge(bn_done, 2 * CH * (g + 1))
                apart()
                for j in range(CH):
                    v.bn_aggr(mv[:, j, :], bn[:, j, :, :].rearrange("p a b -> p (a b)")).then_inc(aggr_done, 1)

            def gn_wait(g, k):
                v.wait_ge(gn_step, GN_STEPS * g + k)

            def chain_mean(g):
                v.wait_ge(mean_ready, g + 1)
                v.tensor_copy(gmean[:], gn_ps[:, 0:CH]).then_inc(gn_step, 1)
                v.tensor_tensor(dev[:], mv[:, :, 0], gn_ps[:, 0:CH], ALU.subtract).then_inc(gn_step, 1)
                gn_wait(g, 2)
                v.tensor_tensor(dev2[:], dev[:], dev[:], ALU.mult).then_inc(gn_step, 1)
                gn_wait(g, 3)
                v.tensor_tensor(vdev[:], dev2[:], mv[:, :, 1], ALU.add).then_inc(gn_step, 1)

            def chain_var(g):
                v.wait_ge(var_ready, g + 1)
                v.tensor_scalar(var_eps[:], gn_ps[:, CH:2 * CH], 1e-5, None, ALU.add).then_inc(gn_step, 1)

            def chain_rstd(g):
                v.wait_ge(sd_done, g + 1)
                v.reciprocal(rs0[:], sd[:]).then_inc(gn_step, 1)
                gn_wait(g, 6)
                v.tensor_tensor(nt[0][:], rs0[:], rs0[:], ALU.mult).then_inc(gn_step, 1)
                gn_wait(g, 7)
                v.tensor_tensor(nt[1][:], nt[0][:], var_eps[:], ALU.mult).then_inc(gn_step, 1)
                gn_wait(g, 8)
                v.tensor_scalar(nt[2][:], nt[1][:], -0.5, 1.5, ALU.mult, ALU.add).then_inc(gn_step, 1)
                gn_wait(g, 9)
                v.scalar_tensor_tensor(out=rstd[:], in0=rs0[:], scalar=ACT_SCALE, in1=nt[2][:],
                                       op0=ALU.mult, op1=ALU.mult).then_inc(gn_step, 1)
                gn_wait(g, 10)

            v.wait_ge(x_in[0], 16 * Q)
            for j in range(CH):
                bn_stats(stage[0][:, j, :], j)
            bn_aggr(0)

            v.wait_ge(par_in, 16 * (10 + 2 * Q))
            step(v.tensor_tensor(raw_i[:, :, 1], raw_i[:, :, 1], mask[:], ALU.mult))
            settle()
            step(v.tensor_reduce(top[:, 0:1], raw_i[:, :, 0:2], AX.XY, ALU.max, apply_absolute_value=True))
            step(v.tensor_reduce(top[:, 1:2], raw_s[:], AX.XY, ALU.max, apply_absolute_value=True))
            step(v.tensor_reduce(top[:, 2:3], raw_c[:, :, 4], AX.X, ALU.max, apply_absolute_value=True))
            for q in range(Q):
                r = slice(32 * q, 32 * q + 32)
                step(v.tensor_reduce(top[r, 3:4], raw_c[r].rearrange("p (n q) k -> p q n k", q=Q)[:, q], AX.XY,
                                     ALU.max, apply_absolute_value=True))
            step(v.tensor_reduce(conv_bias[:], raw_cb[:], AX.X, ALU.add))
            v.tensor_tensor(bsum[:, 0:1], brow[:, 0:1], brow[:, 1:2], ALU.add).then_inc(bias_ready, 1)
            step(v.tensor_tensor(bsum[:, 1:1 + GATES], brow[:, 2:2 + GATES], brow[:, 2 + GATES:2 + 2 * GATES], ALU.add))
            settle()
            step(v.tensor_tensor(top[:, 4:5], top[:, 0:1], top[:, 1:2], ALU.max))
            step(v.tensor_tensor(top[:, 5:6], top[:, 2:3], top[:, 3:4], ALU.max))
            settle()
            step(v.tensor_scalar(top[:, 6:8], top[:, 4:6], 2.0 ** -90, None, ALU.max))
            settle()
            step(v.tensor_scalar(scl[:, 0:2].bitcast(I32), top[:, 6:8].bitcast(I32), EXPONENT_BITS, None, ALU.bitwise_and))
            settle()
            step(v.reciprocal(scl[:, 2:4], scl[:, 0:2]))
            step(v.tensor_scalar(z_unscale[:], scl[:, 0:1], 1.0 / (WEIGHT_TOP * ACT_SCALE), None, ALU.mult))
            step(v.tensor_scalar(y_unscale[:], scl[:, 1:2], 1.0 / (WEIGHT_TOP * ACT_SCALE), None, ALU.mult))
            settle()
            step(v.tensor_scalar(scl[:, 4:6], scl[:, 2:4], WEIGHT_TOP, None, ALU.mult))
            settle()
            def by_residue(t, k):
                return t[:].rearrange("p (n q) k -> p k q n", q=Q)[:, k]

            for k in range(2):
                v.tensor_scalar(turn_i[:, k, :].rearrange("p (q n) -> p q n", q=Q), by_residue(raw_i, k),
                                scl[:, 4:5], None, ALU.mult).then_inc(raws_ready, 1)
            v.tensor_scalar(raw_s[:], raw_s[:], scl[:, 4:5], None, ALU.mult).then_inc(raws_ready, 1)
            for k in range(9):
                v.tensor_scalar(turn_c[:, k, :].rearrange("p (q n) -> p q n", q=Q), by_residue(raw_c, k),
                                scl[:, 5:6], None, ALU.mult).then_inc(raws_ready, 1)
            for n, (hi, lo) in enumerate(((wi_hi, wi_lo), (ws_hi, ws_lo), (wg_hi, wg_lo))):
                v.wait_ge(prep_hi, n + 1)
                high = hi[:].bitcast(F32) if n == 2 else hi[:]
                step(v.tensor_tensor(lo[:], wgroup(n), high, ALU.subtract))
            v.wait_ge(prep_hi, 3 + Q + 1)
            v.wait_ge(wc_zero, 2)
            for q in range(Q):
                step(v.tensor_tensor(diagonal(taps33(wc_lo), q), diagonal(wconv_ps, q),
                                     diagonal(taps33(wc_hi), q), ALU.subtract))
            settle()
            step(v.tensor_tensor(wc_lo[:, 4, :], wconv_ps[:, 1, 1, :], wc_hi[:, 4, :], ALU.subtract))
            v.wait_ge(prep_T, 7)
            step(v.tensor_tensor(gate_bias[:], ps[:, 6, 0:GATES], bsum[:, 1:1 + GATES], ALU.add))

            def norm0(slot, j):
                v.tensor_scalar(stage[slot][:, j, :], stage[slot][:, j, :], gmean[:, j:j + 1], rstd[:, j:j + 1],
                                ALU.subtract, ALU.mult).then_inc(xn0_done, 1)

            def chunk0(i, u, last):
                g = 2 * i + u
                if not last:
                    v.wait_ge(x_in[1 - u], 16 * Q * (i + 1 + u))
                chain_mean(g)
                for j in range(CH):
                    if not last:
                        bn_stats(stage[1 - u][:, j, :], j)
                    if j == 0:
                        chain_var(g)
                    if j == 1:
                        chain_rstd(g)
                    if j >= 1:
                        norm0(u, j - 1)
                norm0(u, CH - 1)
                if not last:
                    bn_aggr(g + 1)

            with v.Fori(0, CHUNKS // 2 - 1) as i:
                chunk0(i, 0, False)
                chunk0(i, 1, False)
            chunk0(CHUNKS // 2 - 1, 0, False)
            chunk0(CHUNKS // 2 - 1, 1, True)

            v.wait_ge(lo0_done, B)
            v.memset(hh[0][:], 0.0).then_inc(hh_done, NB - 1)
            v.memset(hh[1][:], 0.0).then_inc(hh_done, 1)
            v.memset(hl[0][:], 0.0).then_inc(hl_done, NB - 1)
            v.memset(hl[1][:], 0.0).then_inc(hl_done, 1)
            v.memset(cell[:], 0.0).then_inc(c_done, NB)

            def zlow(it, s, k):
                n = width(k)
                v.wait_ge(z_hi_done, it + 1)
                v.scalar_tensor_tensor(out=z_lo[:, 0:n], in0=zbank(s)[:, 0:n], scalar=z_unscale[:],
                                       in1=z_hi[:, 0:n].bitcast(F32), op0=ALU.mult,
                                       op1=ALU.subtract).then_inc(z_lo_done, 1)

            def item(j, s, last):
                u, k = s // NB, s % NB
                it = 2 * NB * j + s
                n = width(k)
                b0, b1 = BLOCKS[k]
                cols = slice(W * b0, W * b1)
                pads = slice(1 + W * b0, 1 + W * b1)
                p = s % 2
                v.wait_ge(gate_done, GATE_BANKS + GATES * it + 3)
                v.tensor_tensor(ig[p][:, 0:n], gate[p][1][:, 0:n], gate[p][2][:, 0:n], ALU.mult).then_inc(ig_done, 1)
                v.wait_ge(ig_done, it + 1)
                v.wait_ge(fc_done, it + 1)
                v.tensor_tensor(cell[:, cols], fc[p][:, 0:n], ig[p][:, 0:n], ALU.add).then_inc(c_done, 1)
                if not last:
                    zlow(it + 1, s + 1, (k + 1) % NB)
                v.wait_ge(tc_done, it + 1)
                v.scalar_tensor_tensor(out=hrow[u][:, cols], in0=gate[p][3][:, 0:n], scalar=ACT_SCALE,
                                       in1=tc[p][:, 0:n], op0=ALU.mult, op1=ALU.mult).then_inc(h_done, 1)
                v.wait_ge(h_done, H_AHEAD + it + 1)
                v.tensor_copy(hh[u][:, pads], hrow[u][:, cols]).then_inc(hh_done, 1)
                v.wait_ge(hh_done, NB + it + 1)
                v.tensor_tensor(hl[u][:, pads], hrow[u][:, cols], hh[u][:, pads], ALU.subtract).then_inc(hl_done, 1)
                v.wait_ge(row_done, it + 1)
                v.transpose(hT[p][:, 0:n], hrow[u][:, cols]).then_inc(ht_done, 1)

            zlow(0, 0, 0)
            with v.Fori(0, H // 2 - 1) as j:
                for s in range(2 * NB):
                    item(j, s, False)
            for s in range(2 * NB):
                item(H // 2 - 1, s, s == 2 * NB - 1)

            def image(b):
                return img32[:, b].rearrange("p h w -> p (h w)")

            def residual(b, j, half_b):
                v.wait_ge(xs_in[j % 2], 16 * Q * (half_b + 1))
                v.scalar_tensor_tensor(out=image(b), in0=image(b), scalar=1.0 / ACT_SCALE, in1=xs[j % 2][:],
                                       op0=ALU.mult, op1=ALU.add).then_inc(x1_done, 1)
                v.wait_ge(x1_done, b + 1)
                apart()
                bn_stats(image(b), j)

            def norm(b, j, free):
                if free:
                    v.wait_ge(lo_done, b - 1)
                v.tensor_scalar(xn[j % 2][:], image(b), gmean[:, j:j + 1], rstd[:, j:j + 1],
                                ALU.subtract, ALU.mult).then_inc(xn_done, 1)

            def add_up(b, j):
                v.wait_ge(y_done, 2 * b + 2)
                v.tensor_tensor(ybuf[j % 2][:], ybuf[j % 2][:], image(b), ALU.add).then_inc(sum_done, 1)

            def chunk1(c, first, last):
                g = CHUNKS + c
                chain_mean(g)
                chain_var(g)
                chain_rstd(g)
                for j in range(CH):
                    b = CH * c + j
                    norm(b, j, not first or j >= 2)
                    if not last:
                        residual(b + CH, j, 2 * c + 2 + j // 2)
                    if not first or j >= 2:
                        add_up(b - 2, j)
                if not last:
                    bn_aggr(g + 1)

            v.wait_ge(row_done, ROW_AHEAD + ITEMS)
            for j in range(CH):
                residual(j, j, j // 2)
            bn_aggr(CHUNKS)
            chunk1(0, True, False)
            with v.Fori(1, CHUNKS - 1) as c:
                chunk1(c, False, False)
            chunk1(CHUNKS - 1, False, True)
            add_up(B - 2, 0)
            add_up(B - 1, 1)

        @block.gpsimd
        def _(pool):
            pool.memset(wc_hi[:], 0.0).then_inc(wc_zero, 1)
            pool.memset(wc_lo[:], 0.0).then_inc(wc_zero, 1)
            pool.sem_inc(gate_done, GATE_BANKS)
            pool.sem_inc(h_done, H_AHEAD)
            pool.sem_inc(z_lo_done, Z_AHEAD)
            pool.sem_inc(row_done, ROW_AHEAD)
            with pool.Fori(0, CHUNKS // 2) as i:
                for u in range(2):
                    for j in range(CH):
                        b = CH * (2 * i + u) + j
                        pool.wait_ge(hi0_done, b + 1)
                        pool.tensor_tensor(img[:, b, :, 1, :], stage[u][:, j, :].rearrange("p (h w) -> p h w", w=W),
                                           img[:, b, :, 0, :], ALU.subtract).then_inc(lo0_done, 1)
            def forget(j, s):
                it = 2 * NB * j + s
                n = width(s % NB)
                b0, b1 = BLOCKS[s % NB]
                pool.wait_ge(c_done, it + 2)
                pool.wait_ge(gate_done, GATE_BANKS + GATES * it + 1)
                pool.tensor_tensor(fc[s % 2][:, 0:n], gate[s % 2][0][:, 0:n], cell[:, W * b0:W * b1],
                                   ALU.mult).then_inc(fc_done, 1)

            def place(j, s):
                b0, b1 = BLOCKS[s % NB]
                pool.wait_ge(ht_done, 2 * NB * j + s + 1)
                pool.wait_ge(par_in, 16)
                pool.tensor_copy(img32[:, b0:b1, 2 * j + s // NB, :],
                                 hT[s % 2][:, 0:width(s % NB)].rearrange("p (b w) -> p b w", w=W)).then_inc(row_done, 1)

            forget(0, 0)
            with pool.Fori(0, H // 2 - 1) as j:
                for s in range(2 * NB):
                    forget(j + (s + 1) // (2 * NB), (s + 1) % (2 * NB))
                    place(j, s)
            for s in range(2 * NB):
                if s < 2 * NB - 1:
                    forget(H // 2 - 1, s + 1)
                place(H // 2 - 1, s)
            pool.wait_ge(row_done, ROW_AHEAD + ITEMS)
            for t in (*pad_hi, *pad_lo):
                pool.memset(t[:], 0.0).then_inc(pads_zero, 1)
            pool.wait_ge(pads_zero, 4)
            with pool.Fori(0, B // 2) as i:
                for u in range(2):
                    pool.wait_ge(hi_done, 2 * i + u + 1)
                    pool.tensor_tensor(interior(pad_lo[u]), xn[u][:].rearrange("p (h w) -> p h w", w=W),
                                       interior(pad_hi[u]), ALU.subtract).then_inc(lo_done, 1)

        @block.scalar
        def _(act):
            for n, hi in enumerate((wi_hi, ws_hi, wg_hi)):
                act.wait_ge(prep_T, n + 1)
                if n == 2:
                    act.copy(wgT[:], wgroup(2)).then_inc(wgt_done, 1)
                act.activation(hi[:], wgroup(n), ACT.Copy).then_inc(prep_hi, 1)
            act.wait_ge(prep_T, 6)
            act.wait_ge(wc_zero, 2)
            for q in range(Q):
                act.activation(diagonal(taps33(wc_hi), q), diagonal(wconv_ps, q), ACT.Copy).then_inc(prep_hi, 1)
            act.wait_ge(prep_hi, 3 + Q)
            act.activation(wc_hi[:, 4, :], wconv_ps[:, 1, 1, :], ACT.Copy).then_inc(prep_hi, 1)

            def square_root(g):
                act.wait_ge(gn_step, GN_STEPS * g + 5)
                act.activation(sd[:], var_eps[:], ACT.Sqrt).then_inc(sd_done, 1)

            with act.Fori(0, CHUNKS // 2) as i:
                for u in range(2):
                    g = 2 * i + u
                    square_root(g)
                    for j in range(CH):
                        b = CH * g + j
                        act.wait_ge(xn0_done, b + 1)
                        act.activation(img[:, b, :, 0, :], stage[u][:, j, :].rearrange("p (h w) -> p h w", w=W),
                                       ACT.Copy).then_inc(hi0_done, 1)

            with act.Fori(0, H // 2) as j:
                for s in range(2 * NB):
                    it = 2 * NB * j + s
                    n = width(s % NB)
                    b0, b1 = BLOCKS[s % NB]
                    p = s % 2
                    act.wait_ge(z_ready, it + 1)
                    act.activation(z_hi[:, 0:n], zbank(s)[:, 0:n], ACT.Identity, scale=z_unscale[:]).then_inc(z_hi_done, 1)
                    act.wait_ge(h_done, it + 1)
                    for m, gt in enumerate(GATE_ORDER):
                        act.wait_ge(gate_ready, GATES * it + m + 1)
                        act.activation(gate[p][m][:, 0:n], gbank(s, m)[:, 0:n],
                                       ACT.Tanh if gt == G_GATE else ACT.Sigmoid,
                                       bias=gate_bias[:, gt:gt + 1]).then_inc(gate_done, 1)
                    act.wait_ge(c_done, NB + it + 1)
                    act.activation(tc[p][:, 0:n], cell[:, W * b0:W * b1], ACT.Tanh).then_inc(tc_done, 1)

            def high(b, j, free):
                act.wait_ge(xn_done, b + 1)
                if free:
                    act.wait_ge(conv_done, 2 * b - 2)
                act.activation(interior(pad_hi[j % 2]), xn[j % 2][:].rearrange("p (h w) -> p h w", w=W),
                               ACT.Copy).then_inc(hi_done, 1)

            def evacuate(b, j, half_b):
                act.wait_ge(stored[j % 2], 16 * Q * half_b)
                for s in range(2):
                    act.wait_ge(conv_done, 2 * b + s + 1)
                    act.activation(ybuf[j % 2][:, 512 * s:512 * s + 512], ps[:, (2 * j + s) % 4, :], ACT.Identity,
                                   bias=conv_bias[:], scale=y_unscale[:]).then_inc(y_done, 1)

            def chunk1(c, first):
                square_root(CHUNKS + c)
                for j in range(CH):
                    b = CH * c + j
                    high(b, j, not first or j >= 2)
                    if not first or j >= 1:
                        evacuate(b - 1, (j - 1) % CH, 2 * c + (j - 1) // 2)

            act.wait_ge(pads_zero, 4)
            chunk1(0, True)
            with act.Fori(1, CHUNKS) as c:
                chunk1(c, False)
            evacuate(B - 1, CH - 1, B // 2 - 1)

        @block.tensor
        def _(pe):
            pe.wait_ge(raws_ready, 2 + 1 + 9)
            for k in range(2):
                ins = pe.transpose(wgroup(0)[:, k, :], turn_i[:, k, :], ident[:])
            ins.then_inc(prep_T, 1)
            for k in range(3):
                ins = pe.transpose(wgroup(1)[:, k, :], raw_s[:, :, k], ident[:])
            ins.then_inc(prep_T, 1)
            for k in range(GATES):
                ins = pe.transpose(wgroup(2)[:, k, :], raw_g[:, k, :], ident[:])
            ins.then_inc(prep_T, 1)
            for d in range(3):
                for e in range(3):
                    ins = pe.transpose(wgroup(3 + d)[:, e, :], turn_c[:, 3 * d + e, :], ident[:])
                ins.then_inc(prep_T, 1)
            pe.wait_ge(wgt_done, 1)
            pe.wait_ge(bias_ready, 1)
            for k in range(GATES):
                ins = pe.matmul(ps[:, 6, k:k + 1], wgT[:, k, :], bsum[:, 0:1], start=True, stop=True)
            ins.then_inc(prep_T, 1)

            def sum_means(g):
                pe.wait_ge(aggr_done, CH * (g + 1))
                pe.matmul(gn_ps[:, 0:CH], group_mean[:], mv[:, :, 0], start=True, stop=True).then_inc(mean_ready, 1)

            def sum_vars(g):
                pe.wait_ge(gn_step, GN_STEPS * g + 4)
                pe.matmul(gn_ps[:, CH:2 * CH], group_mean[:], vdev[:], start=True, stop=True).then_inc(var_ready, 1)

            with pe.Fori(0, CHUNKS) as g:
                sum_means(g)
                sum_vars(g)

            PASSES_I = ((wi_hi, 0), (wi_lo, 0), (wi_hi, 1))

            def input_conv(t, s, k):
                b0, b1 = BLOCKS[k]
                z = zbank(s)[:, 0:width(k)].rearrange("p (b w) -> p b w", w=W)
                for m, (w, half) in enumerate(PASSES_I):
                    pe.matmul(z, w[:, 1, :], img[:, b0:b1, t, half, :], start=(m == 0), stop=False)
                    pe.matmul(z[:, :, 1:W], w[:, 0, :], img[:, b0:b1, t, half, 0:W - 1], start=False, stop=False)

            def item(j, s, last):
                u, k = s // NB, s % NB
                it = 2 * NB * j + s
                b0, b1 = BLOCKS[k]
                n = width(k)
                z = zbank(s)[:, 0:n]
                pe.wait_ge(hh_done, NB * (2 * j + u) + min(k + 2, NB))
                for w in (ws_hi, ws_lo):
                    for tap in range(3):
                        pe.matmul(z, w[:, tap, :], hh[1 - u][:, W * b0 + tap:W * b1 + tap], start=False, stop=False)
                pe.wait_ge(hl_done, NB * (2 * j + u) + min(k + 2, NB))
                for tap in range(3):
                    ins = pe.matmul(z, ws_hi[:, tap, :], hl[1 - u][:, W * b0 + tap:W * b1 + tap],
                                    start=False, stop=(tap == 2))
                ins.then_inc(z_ready, 1)
                if not last:
                    pe.wait_ge(z_lo_done, it + 1)
                    input_conv(2 * j + (s + 1) // NB, s + 1, (k + 1) % NB)
                pe.wait_ge(z_hi_done, it + 1)
                for m in range(2):
                    pe.wait_ge(gate_done, GATES * it + m + 1)
                    pe.matmul(gbank(s, m)[:, 0:n], wg_hi[:, GATE_ORDER[m], :], z_hi[:, 0:n], start=True, stop=False)
                    pe.matmul(gbank(s, m)[:, 0:n], wg_lo[:, GATE_ORDER[m], :], z_hi[:, 0:n], start=False, stop=False)
                pe.wait_ge(z_lo_done, Z_AHEAD + it + 1)
                for m in range(2):
                    pe.matmul(gbank(s, m)[:, 0:n], wg_hi[:, GATE_ORDER[m], :], z_lo[:, 0:n],
                              start=False, stop=True).then_inc(gate_ready, 1)
                for m in range(2, GATES):
                    pe.wait_ge(gate_done, GATES * it + m + 1)
                    pe.matmul(gbank(s, m)[:, 0:n], wg_hi[:, GATE_ORDER[m], :], z_hi[:, 0:n], start=True, stop=False)
                    pe.matmul(gbank(s, m)[:, 0:n], wg_lo[:, GATE_ORDER[m], :], z_hi[:, 0:n], start=False, stop=False)
                    pe.matmul(gbank(s, m)[:, 0:n], wg_hi[:, GATE_ORDER[m], :], z_lo[:, 0:n],
                              start=False, stop=True).then_inc(gate_ready, 1)

            pe.wait_ge(lo0_done, B)
            input_conv(0, 0, 0)
            pe.wait_ge(hh_done, NB)
            pe.wait_ge(hl_done, NB)
            with pe.Fori(0, H // 2 - 1) as j:
                for s in range(2 * NB):
                    item(j, s, False)
            for s in range(2 * NB):
                item(H // 2 - 1, s, s == 2 * NB - 1)

            def conv_half(b, j, s, free):
                y = ps[:, (2 * j + s) % 4, :].rearrange("p (h w) -> p h w", w=W)
                if free:
                    pe.wait_ge(y_done, 2 * b + s - 3)
                order = [(w, t, d, e) for w, t in ((wc_hi, pad_hi), (wc_lo, pad_hi), (wc_hi, pad_lo))
                         for d in range(3) for e in range(3)]
                for m, (w, t, d, e) in enumerate(order):
                    ins = pe.matmul(y, w[:, 3 * d + e, :], padded(t[j % 2], s, d - 1, e - 1),
                                    start=(m == 0), stop=(m == len(order) - 1))
                ins.then_inc(conv_done, 1)

            def chunk1(c, first, last):
                for j in range(CH):
                    b = CH * c + j
                    pe.wait_ge(lo_done, b + 1)
                    for s in range(2):
                        if j == CH - 1 and not last:
                            (sum_means if s == 0 else sum_vars)(CHUNKS + c + 1)
                        conv_half(b, j, s, not first or j >= 2)

            sum_means(CHUNKS)
            sum_vars(CHUNKS)
            chunk1(0, True, False)
            with pe.Fori(1, CHUNKS - 1) as c:
                chunk1(c, False, False)
            chunk1(CHUNKS - 1, False, True)


_INS = ["x", "L0_conv_w_i2s", "L0_conv_b_i2s", "L0_conv_w_s2s", "L0_conv_b_s2s", "L0_conv_w_ih", "L0_conv_b_ih",
        "L0_conv_b_hh", "L1_conv_W", "L1_conv_b"]


def shape_constants():
    c = np.arange(P)
    same_group = (c[:, None] % 32 == c[None, :] % 32).astype(np.float32) / Q
    kept = (c[:, None] % 3 >= c[None, :] % 3).astype(np.float32)
    return np.stack([np.eye(P, dtype=np.float32), same_group, kept])


def kernel(**inputs):
    import concourse.bacc as _bacc
    from concourse.bass_utils import run_bass_kernel_spmd as _run

    nc = _bacc.Bacc("TRN2", target_bir_lowering=False, num_devices=1)
    arrays, args = {}, []
    for name in _INS:
        a = np.ascontiguousarray(inputs[name])
        arrays[f"in_{name}_dram"] = a
        args.append(nc.dram_tensor(f"in_{name}_dram", a.shape, mybir.dt.from_np(a.dtype), kind="ExternalInput").ap())
    arrays["in_consts_dram"] = shape_constants()
    args.append(nc.dram_tensor("in_consts_dram", (3, P, P), F32, kind="ExternalInput").ap())
    out = nc.dram_tensor("out_0_dram", (B, P, H, W), F32, kind="ExternalOutput").ap()
    build_network(nc, *args, out)
    r = _run(nc, [arrays], core_ids=[0])
    return r.results[0]["out_0_dram"]
```

```python
from contextlib import ExitStack

import numpy as np
import concourse.bass as bass
from concourse import mybir

F32 = mybir.dt.float32
F32R = mybir.dt.float32r
F16 = mybir.dt.float16
I32 = mybir.dt.int32
ALU = mybir.AluOpType
ACT = mybir.ActivationFunctionType
AX = mybir.AxisListType

P = 128
B, H, W = 32, 32, 32
HW = H * W
Q = 4
GATES = 4

ACT_SCALE = 512.0
WEIGHT_TOP = 4096.0
EXPONENT_BITS = 0x7F800000

BLOCKS = [(0, 11), (11, 21), (21, 32)]
NB = len(BLOCKS)
ITEMS = NB * H
F_GATE, I_GATE, G_GATE, O_GATE = 1, 0, 2, 3
GATE_ORDER = [F_GATE, I_GATE, G_GATE, O_GATE]
GATE_BANKS = 6

CH = 4
CHUNKS = B // CH
GN_STEPS = 11

H_AHEAD = 2
PARAMETERS = 12
Z_AHEAD = 1
ROW_AHEAD = 2
PAD_BUFFERS = 6


def width(k):
    return W * (BLOCKS[k][1] - BLOCKS[k][0])


PADW = W + 1
PADN = 1 + (H + 2) * PADW + 1


def build_network(nc, x, w_i2s, b_i2s, w_s2s, b_s2s, w_ih, b_ih, b_hh, w_conv, b_conv, consts, out):
    x_q = x.rearrange("b (n q) h w -> q n b (h w)", q=Q)
    out_q = out.rearrange("b (n q) h w -> q n b (h w)", q=Q)

    with ExitStack() as ctx:
        def sb(name, shape, dt, stack=ctx):
            return stack.enter_context(nc.sbuf_tensor(name, shape, dt))

        def sem(name):
            return ctx.enter_context(nc.semaphore(name))

        img = sb("img", [P, B, H, 2, W], F16)
        img32 = img[:].rearrange("p b h s w -> p (b h s w)").bitcast(F32).rearrange("p (b h w) -> p b h w", b=B, h=H)
        ident = sb("ident", [P, P], F32)
        group_mean = sb("group_mean", [P, P], F32)
        wi_hi = sb("wi_hi", [P, 2, P], F16)
        wi_lo = sb("wi_lo", [P, 2, P], F16)
        ws_hi = sb("ws_hi", [P, 3, P], F16)
        ws_lo = sb("ws_lo", [P, 3, P], F16)
        wg_hi = sb("wg_hi", [P, GATES, P], F32R)
        wg_lo = sb("wg_lo", [P, GATES, P], F32R)
        wc_hi = sb("wc_hi", [P, 9, P], F16)
        wc_lo = sb("wc_lo", [P, P], F16)
        wt_hi = sb("wt_hi", [P, 3, Q, 32], F16)
        wt_lo = sb("wt_lo", [P, 3, Q, 32], F16)
        z_unscale = sb("z_unscale", [P, 1], F32)
        y_unscale = sb("y_unscale", [P, 1], F32)
        gate_bias = sb("gate_bias", [P, GATES], F32)
        conv_bias = sb("conv_bias", [P, 1], F32)
        bn = sb("bn", [P, CH, 2, 6], F32)
        mv = sb("mv", [P, CH, 2], F32)
        gmean = sb("gmean", [P, CH], F32)
        dev = sb("dev", [P, CH], F32)
        dev2 = sb("dev2", [P, CH], F32)
        vdev = sb("vdev", [P, CH], F32)
        warm = sb("warm", [P, 4], F32)
        var_eps = sb("var_eps", [P, CH], F32)
        sd = sb("sd", [P, CH], F32)
        rs0 = sb("rs0", [P, CH], F32)
        nt = [sb(f"nt{i}", [P, CH], F32) for i in range(3)]
        rstd = sb("rstd", [P, CH], F32)
        nbias = sb("nbias", [P, CH], F32)

        with ExitStack() as s0:
            xn0 = [sb(f"xn0{i}", [P, HW], F32, s0) for i in range(CH)]
            raw_i = sb("raw_i", [P, P, 3], F32, s0)
            raw_s = sb("raw_s", [P, P, 3], F32, s0)
            raw_g = sb("raw_g", [P, GATES, P], F32, s0)
            raw_c = sb("raw_c", [P, P, 9], F32, s0)
            turn_i = sb("turn_i", [P, 2, P], F32, s0)
            turn_c = sb("turn_c", [P, 9, P], F32, s0)
            raw_cb = sb("raw_cb", [P, P], F32, s0)
            mask = sb("mask", [P, P], F32, s0)
            wgT = sb("wgT", [P, GATES, P], F32, s0)
            brow = sb("brow", [P, 2 + 2 * GATES], F32, s0)
            bsum = sb("bsum", [P, 1 + GATES], F32, s0)
            top = sb("top", [P, 8], F32, s0)
            scl = sb("scl", [P, 6], F32, s0)
        with ExitStack() as s1:
            cell = sb("cell", [P, B * W], F32, s1)
            hrow = [sb(f"hrow{i}", [P, B * W], F32, s1) for i in range(2)]
            hh = [sb(f"hh{i}", [P, B * W + 2], F16, s1) for i in range(2)]
            hl = [sb(f"hl{i}", [P, B * W + 2], F16, s1) for i in range(2)]
            gate = [[sb(f"gate{i}{j}", [P, 352], F32, s1) for j in range(GATES)] for i in range(2)]
            fc = [sb(f"fc{i}", [P, 352], F32, s1) for i in range(2)]
            ig = [sb(f"ig{i}", [P, 352], F32, s1) for i in range(2)]
            hT = [sb(f"hT{i}", [P, 352], F32, s1) for i in range(2)]
            tc = [sb(f"tc{i}", [P, 352], F32, s1) for i in range(2)]
            z_hi = sb("z_hi", [P, 352], F32R, s1)
            z_lo = sb("z_lo", [P, 352], F32R, s1)
        with ExitStack() as s2:
            xs = [sb(f"xs{i}", [P, HW], F32, s2) for i in range(CH)]
            xn = [sb(f"xn{i}", [P, HW], F32, s2) for i in range(2)]
            pad_hi = [sb(f"pad_hi{i}", [P, PADN], F16, s2) for i in range(2)]
            pad_lo = [sb(f"pad_lo{i}", [P, PADN], F16, s2) for i in range(2)]
            shifted = [sb(f"shifted{i}", [P, Q, PADN], F16, s2) for i in range(2)]
            ybuf = [sb(f"ybuf{i}", [P, HW], F32, s2) for i in range(2)]

        ps = ctx.enter_context(nc.psum_tensor("ps", [P, 8, 512], F32))

        par_in = sem("par_in")
        x_in = [sem(f"x_in{i}") for i in range(2)]
        prep = sem("prep")
        scales_ready = sem("scales_ready")
        raws_ready = sem("raws_ready")
        bias_ready = sem("bias_ready")
        prep_T = sem("prep_T")
        wgt_done = sem("wgt_done")
        prep_wt = sem("prep_wt")
        prep_hi = sem("prep_hi")
        warm_set = sem("warm_set")
        warmed = sem("warmed")
        waited = sem("waited")
        bn_done = sem("bn_done")
        aggr_done = sem("aggr_done")
        mean_ready = sem("mean_ready")
        var_ready = sem("var_ready")
        gn_step = sem("gn_step")
        sd_done = sem("sd_done")
        xn0_done = sem("xn0_done")
        xn0v_done = sem("xn0v_done")
        hi0_done = sem("hi0_done")
        lo0_done = sem("lo0_done")
        lo0v_done = sem("lo0v_done")
        z_ready = sem("z_ready")
        z_hi_done = sem("z_hi_done")
        z_lo_done = sem("z_lo_done")
        gate_ready = sem("gate_ready")
        gate_done = sem("gate_done")
        fc_done = sem("fc_done")
        ig_done = sem("ig_done")
        c_done = sem("c_done")
        tc_done = sem("tc_done")
        h_done = sem("h_done")
        hh_done = sem("hh_done")
        hl_done = sem("hl_done")
        wc_zero = sem("wc_zero")
        ht_done = sem("ht_done")
        row_done = sem("row_done")
        xs_in = [sem(f"xs_in{i}") for i in range(CH)]
        x1_done = sem("x1_done")
        pads_zero = sem("pads_zero")
        shifted_in = [sem(f"shifted_in{i}") for i in range(2)]
        unshifted_done = sem("unshifted_done")
        xn_done = sem("xn_done")
        hi_done = sem("hi_done")
        lo_done = sem("lo_done")
        conv_done = sem("conv_done")
        y_done = sem("y_done")
        sum_done = sem("sum_done")
        stored = [sem(f"stored{i}") for i in range(2)]

        block = ctx.enter_context(nc.Block())

        def zbank(it):
            return ps[:, it % 2, :]

        def gbank(it, n):
            return ps[:, 2 + (GATES * it + n) % GATE_BANKS, :]

        gn_ps = ps[:, 7, 0:2 * CH]

        def padded(t, half, dh, dw):
            at = 1 + (16 * half + 1 + dh) * PADW + dw
            return t[:, at:at + 16 * PADW].rearrange("p (h w) -> p h w", w=PADW)[:, :, 0:W]

        def interior(t):
            return t[:, 1 + PADW:1 + PADW + H * PADW].rearrange("p (h w) -> p h w", w=PADW)[:, :, 0:W]

        def wgroup(n):
            return ps[:, n, 0:[2, 3, 4, 3, 3, 3][n] * P].rearrange("p (a b) -> p a b", b=P)

        wconv_ps = ps[:, 3:6, 0:3 * P].rearrange("p d (e o) -> p d e o", o=P)

        def diagonal(t, q):
            return t[32 * q:32 * q + 32, :, :, 32 * q:32 * q + 32]

        def taps33(t):
            return t[:].rearrange("p (d e) o -> p d e o", e=3)

        WT_PARTS = ((0, slice(0, 3)), (1, slice(0, 3, 2)), (2, slice(0, 3)))

        def wt_block(t, e, rows, q):
            return t[32 * e:32 * e + 32, rows, q, :]

        def wt_source(e, rows, q):
            return wconv_ps[32 * q:32 * q + 32, rows, e, 32 * q:32 * q + 32]

        @block.sync
        def _(sp):
            def load_chunk(g):
                for b in range(CH * g, CH * g + CH):
                    sp.dma_start(img32[:, b].rearrange("p h w -> p (h w)"), x_q[:, :, b, :]).then_inc(x_in[g % 2], 16)

            load_chunk(0)
            sp.dma_start(raw_i[:], w_i2s.rearrange("o i a k -> o i (a k)")).then_inc(par_in, 16)
            sp.dma_start(raw_s[:], w_s2s.rearrange("o i a k -> o i (a k)")).then_inc(par_in, 16)
            sp.dma_start(raw_g[:], w_ih.rearrange("(j p) s -> p j s", p=P)).then_inc(par_in, 16)
            for n, t in enumerate((ident, group_mean, mask)):
                sp.dma_start(t[:], consts[n]).then_inc(par_in, 16)
            with nc.allow_non_contiguous_dma(reason="bias columns"):
                sp.dma_start(brow[:, 0:1], b_i2s.rearrange("(p a) -> p a", a=1)).then_inc(par_in, 16)
                sp.dma_start(brow[:, 1:2], b_s2s.rearrange("(p a) -> p a", a=1)).then_inc(par_in, 16)
                sp.dma_start(brow[:, 2:2 + GATES], b_ih.rearrange("(j p) -> p j", p=P)).then_inc(par_in, 16)
                sp.dma_start(brow[:, 2 + GATES:2 + 2 * GATES], b_hh.rearrange("(j p) -> p j", p=P)).then_inc(par_in, 16)
            sp.dma_start(raw_c[:].rearrange("p i k -> p (i k)"), w_conv.rearrange("(n q) i a k -> q n (i a k)", q=Q)).then_inc(par_in, 16)
            sp.dma_start(raw_cb[:], b_conv.rearrange("(n q) i -> q n i", q=Q)).then_inc(par_in, 16)
            load_chunk(1)
            for g in range(2, CHUNKS):
                sp.wait_ge(x_in[g % 2], 16 * CH * (g // 2))
                load_chunk(g)

            def shift(b, slot):
                sp.wait_ge(hi_done, b + 1)
                for e in (0, 2):
                    for q in range(Q):
                        sp.dma_start(shifted[slot][32 * e:32 * e + 32, q, 1:PADN - 1],
                                     pad_hi[slot][32 * q:32 * q + 32, e:e + PADN - 2]).then_inc(shifted_in[slot], 16)

            def store(b, slot):
                sp.wait_ge(sum_done, b + 1)
                sp.dma_start(out_q[:, :, b, :], ybuf[slot][:]).then_inc(stored[slot], 16)

            def load_xs(b, slot):
                sp.dma_start(xs[slot][:], x_q[:, :, b, :]).then_inc(xs_in[slot], 16)

            def chunk1(c, first, ahead):
                for j in range(CH):
                    shift(CH * c + j, j % 2)
                    if ahead:
                        sp.wait_ge(x1_done, CH * (c + 1) + j + 1)
                        load_xs(CH * (c + 2) + j, j)
                    if not first or j >= 2:
                        store(CH * c + j - 2, j % 2)

            sp.wait_ge(row_done, ROW_AHEAD + ITEMS)
            for j in range(CH):
                load_xs(j, j)
            for j in range(CH):
                sp.wait_ge(x1_done, j + 1)
                load_xs(CH + j, j)
            sp.wait_ge(pads_zero, PAD_BUFFERS)
            chunk1(0, True, True)
            with sp.Fori(1, CHUNKS - 2) as c:
                chunk1(c, False, True)
            for c in range(CHUNKS - 2, CHUNKS):
                chunk1(c, False, False)
            for b in range(B - 2, B):
                store(b, b % 2)
            for u in range(2):
                sp.wait_ge(stored[u], 16 * (B // 2))

        @block.vector
        def _(v):
            n_prep = [0]

            def step(ins):
                n_prep[0] += 1
                ins.then_inc(prep, 1)

            def settle():
                v.wait_ge(prep, n_prep[0])

            def image(b):
                return img32[:, b].rearrange("p h w -> p (h w)")

            def apart():
                v.sem_inc(waited, 1)

            def bn_stats(src, j):
                for s in range(2):
                    v.bn_stats(bn[:, j, s, :], src[:, 512 * s:512 * s + 512]).then_inc(bn_done, 1)

            def bn_aggr(g):
                v.wait_ge(bn_done, 2 * CH * (g + 1))
                apart()
                for j in range(CH):
                    v.bn_aggr(mv[:, j, :], bn[:, j, :, :].rearrange("p a b -> p (a b)")).then_inc(aggr_done, 1)

            def gn_wait(g, k):
                v.wait_ge(gn_step, GN_STEPS * g + k)

            def chain_mean(g):
                v.wait_ge(mean_ready, g + 1)
                v.tensor_copy(gmean[:], gn_ps[:, 0:CH]).then_inc(gn_step, 1)
                v.tensor_tensor(dev[:], mv[:, :, 0], gn_ps[:, 0:CH], ALU.subtract).then_inc(gn_step, 1)
                gn_wait(g, 2)
                v.tensor_tensor(dev2[:], dev[:], dev[:], ALU.mult).then_inc(gn_step, 1)
                gn_wait(g, 3)
                v.tensor_tensor(vdev[:], dev2[:], mv[:, :, 1], ALU.add).then_inc(gn_step, 1)

            def chain_var(g):
                v.wait_ge(var_ready, g + 1)
                v.tensor_scalar(var_eps[:], gn_ps[:, CH:2 * CH], 1e-5, None, ALU.add).then_inc(gn_step, 1)

            def chain_rstd(g):
                v.wait_ge(sd_done, g + 1)
                v.reciprocal(rs0[:], sd[:]).then_inc(gn_step, 1)
                gn_wait(g, 6)
                v.tensor_tensor(nt[0][:], rs0[:], rs0[:], ALU.mult).then_inc(gn_step, 1)
                gn_wait(g, 7)
                v.tensor_tensor(nt[1][:], nt[0][:], var_eps[:], ALU.mult).then_inc(gn_step, 1)
                gn_wait(g, 8)
                v.tensor_scalar(nt[2][:], nt[1][:], -0.5, 1.5, ALU.mult, ALU.add).then_inc(gn_step, 1)
                gn_wait(g, 9)
                v.scalar_tensor_tensor(out=rstd[:], in0=rs0[:], scalar=ACT_SCALE, in1=nt[2][:],
                                       op0=ALU.mult, op1=ALU.mult).then_inc(gn_step, 1)
                gn_wait(g, 10)
                v.scalar_tensor_tensor(out=nbias[:], in0=gmean[:], scalar=-1.0, in1=rstd[:],
                                       op0=ALU.mult, op1=ALU.mult).then_inc(gn_step, 1)

            v.wait_ge(x_in[0], 16 * CH)
            for j in range(CH):
                bn_stats(image(j), j)
            bn_aggr(0)

            v.wait_ge(par_in, 16 * PARAMETERS)
            step(v.tensor_tensor(raw_i[:, :, 1], raw_i[:, :, 1], mask[:], ALU.mult))
            settle()
            step(v.tensor_reduce(top[:, 0:1], raw_i[:, :, 0:2], AX.XY, ALU.max, apply_absolute_value=True))
            step(v.tensor_reduce(top[:, 1:2], raw_s[:], AX.XY, ALU.max, apply_absolute_value=True))
            step(v.tensor_reduce(top[:, 2:3], raw_c[:, :, 4], AX.X, ALU.max, apply_absolute_value=True))
            for q in range(Q):
                r = slice(32 * q, 32 * q + 32)
                step(v.tensor_reduce(top[r, 3:4], raw_c[r].rearrange("p (n q) k -> p q n k", q=Q)[:, q], AX.XY,
                                     ALU.max, apply_absolute_value=True))
            step(v.tensor_reduce(conv_bias[:], raw_cb[:], AX.X, ALU.add))
            v.tensor_tensor(bsum[:, 0:1], brow[:, 0:1], brow[:, 1:2], ALU.add).then_inc(bias_ready, 1)
            step(v.tensor_tensor(bsum[:, 1:1 + GATES], brow[:, 2:2 + GATES], brow[:, 2 + GATES:2 + 2 * GATES], ALU.add))
            settle()
            step(v.tensor_tensor(top[:, 4:5], top[:, 0:1], top[:, 1:2], ALU.max))
            step(v.tensor_tensor(top[:, 5:6], top[:, 2:3], top[:, 3:4], ALU.max))
            settle()
            step(v.tensor_scalar(top[:, 6:8], top[:, 4:6], 2.0 ** -90, None, ALU.max))
            settle()
            step(v.tensor_scalar(scl[:, 0:2].bitcast(I32), top[:, 6:8].bitcast(I32), EXPONENT_BITS, None, ALU.bitwise_and))
            settle()
            step(v.reciprocal(scl[:, 2:4], scl[:, 0:2]))
            step(v.tensor_scalar(z_unscale[:], scl[:, 0:1], 1.0 / (WEIGHT_TOP * ACT_SCALE), None, ALU.mult))
            step(v.tensor_scalar(y_unscale[:], scl[:, 1:2], 1.0 / (WEIGHT_TOP * ACT_SCALE), None, ALU.mult))
            settle()
            v.tensor_scalar(scl[:, 4:6], scl[:, 2:4], WEIGHT_TOP, None, ALU.mult).then_inc(scales_ready, 1)

            def low_weights():
                for n, (hi, lo) in enumerate(((wi_hi, wi_lo), (ws_hi, ws_lo), (wg_hi, wg_lo))):
                    v.wait_ge(prep_hi, n + 1)
                    high = hi[:].bitcast(F32) if n == 2 else hi[:]
                    step(v.tensor_tensor(lo[:], wgroup(n), high, ALU.subtract))
                v.wait_ge(prep_hi, 3 + Q + 1)
                step(v.tensor_tensor(wc_lo[:], wconv_ps[:, 1, 1, :], wc_hi[:, 4, :], ALU.subtract))
                v.wait_ge(prep_wt, Q * len(WT_PARTS))
                for q in range(Q):
                    for e, rows in WT_PARTS:
                        step(v.tensor_tensor(wt_block(wt_lo, e, rows, q), wt_source(e, rows, q),
                                             wt_block(wt_hi, e, rows, q), ALU.subtract))
                v.wait_ge(prep_T, 7)
                step(v.tensor_tensor(gate_bias[:], ps[:, 6, 0:GATES], bsum[:, 1:1 + GATES], ALU.add))

            def low_image(g):
                v.wait_ge(hi0_done, CH * g + 1)
                v.tensor_tensor(img[:, CH * g, :, 1, :], xn0[0][:].rearrange("p (h w) -> p h w", w=W),
                                img[:, CH * g, :, 0, :], ALU.subtract).then_inc(lo0v_done, 1)

            def norm_image(g):
                v.tensor_scalar(xn0[0][:], image(CH * g), gmean[:, 0:1], rstd[:, 0:1],
                                ALU.subtract, ALU.mult).then_inc(xn0v_done, 1)

            def chunk0(i, u, first, last):
                g = 2 * i + u
                if not first:
                    low_image(g - 1)
                chain_mean(g)
                if not last:
                    v.wait_ge(x_in[1 - u], 16 * CH * (i + 1 + u))
                    apart()
                for j in range(CH):
                    if not last:
                        bn_stats(image(CH * (g + 1) + j), j)
                    if j == 0:
                        chain_var(g)
                    if j == 1:
                        chain_rstd(g)
                        norm_image(g)
                if not last:
                    bn_aggr(g + 1)

            chunk0(0, 0, True, False)
            chunk0(0, 1, False, False)
            with v.Fori(1, CHUNKS // 2 - 1) as i:
                chunk0(i, 0, False, False)
                chunk0(i, 1, False, False)
            low_weights()
            chunk0(CHUNKS // 2 - 1, 0, False, False)
            chunk0(CHUNKS // 2 - 1, 1, False, True)
            low_image(CHUNKS - 1)

            v.wait_ge(lo0_done, (CH - 1) * (CHUNKS + 1))
            v.wait_ge(lo0v_done, CHUNKS)
            v.memset(hh[0][:], 0.0).then_inc(hh_done, NB - 1)
            v.memset(hh[1][:], 0.0).then_inc(hh_done, 1)
            v.memset(hl[0][:], 0.0).then_inc(hl_done, NB - 1)
            v.memset(hl[1][:], 0.0).then_inc(hl_done, 1)
            v.memset(cell[:], 0.0).then_inc(c_done, NB)

            def zlow(it, s, k):
                n = width(k)
                v.wait_ge(z_hi_done, it + 1)
                v.scalar_tensor_tensor(out=z_lo[:, 0:n], in0=zbank(s)[:, 0:n], scalar=z_unscale[:],
                                       in1=z_hi[:, 0:n].bitcast(F32), op0=ALU.mult,
                                       op1=ALU.subtract).then_inc(z_lo_done, 1)

            def item(j, s, last):
                u, k = s // NB, s % NB
                it = 2 * NB * j + s
                n = width(k)
                b0, b1 = BLOCKS[k]
                cols = slice(W * b0, W * b1)
                pads = slice(1 + W * b0, 1 + W * b1)
                p = s % 2
                v.wait_ge(gate_done, GATE_BANKS + GATES * it + 3)
                v.tensor_tensor(ig[p][:, 0:n], gate[p][1][:, 0:n], gate[p][2][:, 0:n], ALU.mult).then_inc(ig_done, 1)
                v.wait_ge(ig_done, it + 1)
                v.wait_ge(fc_done, it + 1)
                v.tensor_tensor(cell[:, cols], fc[p][:, 0:n], ig[p][:, 0:n], ALU.add).then_inc(c_done, 1)
                if not last:
                    zlow(it + 1, s + 1, (k + 1) % NB)
                v.wait_ge(tc_done, it + 1)
                v.scalar_tensor_tensor(out=hrow[u][:, cols], in0=gate[p][3][:, 0:n], scalar=ACT_SCALE,
                                       in1=tc[p][:, 0:n], op0=ALU.mult, op1=ALU.mult).then_inc(h_done, 1)
                v.wait_ge(h_done, H_AHEAD + it + 1)
                v.tensor_copy(hh[u][:, pads], hrow[u][:, cols]).then_inc(hh_done, 1)
                v.wait_ge(hh_done, NB + it + 1)
                v.tensor_tensor(hl[u][:, pads], hrow[u][:, cols], hh[u][:, pads], ALU.subtract).then_inc(hl_done, 1)
                v.wait_ge(row_done, it + 1)
                v.transpose(hT[p][:, 0:n], hrow[u][:, cols]).then_inc(ht_done, 1)

            zlow(0, 0, 0)
            with v.Fori(0, H // 2 - 1) as j:
                for s in range(2 * NB):
                    item(j, s, False)
            for s in range(2 * NB):
                item(H // 2 - 1, s, s == 2 * NB - 1)

            def residual(c, j):
                b = CH * c + j
                v.wait_ge(xs_in[j], 16 * (c + 1))
                v.scalar_tensor_tensor(out=image(b), in0=image(b), scalar=1.0 / ACT_SCALE, in1=xs[j][:],
                                       op0=ALU.mult, op1=ALU.add).then_inc(x1_done, 1)
                v.wait_ge(x1_done, b + 1)
                apart()
                bn_stats(image(b), j)

            def norm(b, j, free):
                if free:
                    v.wait_ge(lo_done, b - 1)
                v.tensor_scalar(xn[j % 2][:], image(b), gmean[:, j:j + 1], rstd[:, j:j + 1],
                                ALU.subtract, ALU.mult).then_inc(xn_done, 1)

            def unshifted(b, j):
                v.wait_ge(hi_done, b + 1)
                for q in range(Q):
                    v.tensor_copy(shifted[j % 2][32:64, q, :], pad_hi[j % 2][32 * q:32 * q + 32, :]).then_inc(unshifted_done, 1)

            def add_up(b, j):
                v.wait_ge(y_done, 2 * b + 2)
                v.tensor_tensor(ybuf[j % 2][:], ybuf[j % 2][:], image(b), ALU.add).then_inc(sum_done, 1)

            def chunk1(c, first, last):
                g = CHUNKS + c
                for j in range(CH):
                    b = CH * c + j
                    norm(b, j, not first or j >= 2)
                    if not last:
                        for k in (2 * j, 2 * j + 1):
                            if k < CH:
                                residual(c + 1, k)
                        if j == 1:
                            bn_aggr(g + 1)
                        if j == CH - 1:
                            v.wait_ge(xn_done, CH * (c + 1))
                            chain_mean(g + 1)
                            chain_var(g + 1)
                    unshifted(b, j)
                    if not first or j >= 2:
                        add_up(b - 2, j)
                if not last:
                    chain_rstd(g + 1)

            v.wait_ge(row_done, ROW_AHEAD + ITEMS)
            for j in range(CH):
                residual(0, j)
            bn_aggr(CHUNKS)
            chain_mean(CHUNKS)
            chain_var(CHUNKS)
            chain_rstd(CHUNKS)
            chunk1(0, True, False)
            with v.Fori(1, CHUNKS - 1) as c:
                chunk1(c, False, False)
            chunk1(CHUNKS - 1, False, True)
            add_up(B - 2, 0)
            add_up(B - 1, 1)

        @block.gpsimd
        def _(pool):
            pool.memset(warm[:], 1.0).then_inc(warm_set, 1)
            pool.memset(wc_hi[:], 0.0).then_inc(wc_zero, 1)
            for t in (wt_hi, wt_lo):
                pool.memset(t[:], 0.0).then_inc(wc_zero, 1)
            pool.sem_inc(gate_done, GATE_BANKS)
            pool.sem_inc(h_done, H_AHEAD)
            pool.sem_inc(z_lo_done, Z_AHEAD)
            pool.sem_inc(row_done, ROW_AHEAD)
            pool.sem_inc(lo0_done, CH - 1)

            def by_residue(t, k):
                return t[:].rearrange("p (n q) k -> p k q n", q=Q)[:, k]

            pool.wait_ge(scales_ready, 1)
            for k in range(2):
                pool.tensor_scalar(turn_i[:, k, :].rearrange("p (q n) -> p q n", q=Q), by_residue(raw_i, k),
                                   scl[:, 4:5], None, ALU.mult).then_inc(raws_ready, 1)
            pool.tensor_scalar(raw_s[:], raw_s[:], scl[:, 4:5], None, ALU.mult).then_inc(raws_ready, 1)
            for k in range(9):
                pool.tensor_scalar(turn_c[:, k, :].rearrange("p (q n) -> p q n", q=Q), by_residue(raw_c, k),
                                   scl[:, 5:6], None, ALU.mult).then_inc(raws_ready, 1)

            with pool.Fori(0, CHUNKS) as g:
                for j in range(1, CH):
                    b = CH * g + j
                    pool.wait_ge(hi0_done, b + 1)
                    pool.tensor_tensor(img[:, b, :, 1, :], xn0[j][:].rearrange("p (h w) -> p h w", w=W),
                                       img[:, b, :, 0, :], ALU.subtract).then_inc(lo0_done, 1)

            def forget(j, s):
                it = 2 * NB * j + s
                n = width(s % NB)
                b0, b1 = BLOCKS[s % NB]
                pool.wait_ge(c_done, it + 2)
                pool.wait_ge(gate_done, GATE_BANKS + GATES * it + 1)
                pool.tensor_tensor(fc[s % 2][:, 0:n], gate[s % 2][0][:, 0:n], cell[:, W * b0:W * b1],
                                   ALU.mult).then_inc(fc_done, 1)

            def place(j, s):
                b0, b1 = BLOCKS[s % NB]
                pool.wait_ge(ht_done, 2 * NB * j + s + 1)
                pool.wait_ge(par_in, 16)
                pool.tensor_copy(img32[:, b0:b1, 2 * j + s // NB, :],
                                 hT[s % 2][:, 0:width(s % NB)].rearrange("p (b w) -> p b w", w=W)).then_inc(row_done, 1)

            forget(0, 0)
            with pool.Fori(0, H // 2 - 1) as j:
                for s in range(2 * NB):
                    forget(j + (s + 1) // (2 * NB), (s + 1) % (2 * NB))
                    place(j, s)
            for s in range(2 * NB):
                if s < 2 * NB - 1:
                    forget(H // 2 - 1, s + 1)
                place(H // 2 - 1, s)
            pool.wait_ge(row_done, ROW_AHEAD + ITEMS)
            for t in (*pad_hi, *pad_lo):
                pool.memset(t[:], 0.0).then_inc(pads_zero, 1)
            pool.wait_ge(pads_zero, 4)
            for t in shifted:
                pool.memset(t[3 * 32:P], 0.0).then_inc(pads_zero, 1)
            pool.wait_ge(pads_zero, PAD_BUFFERS)
            with pool.Fori(0, B // 2) as i:
                for u in range(2):
                    pool.wait_ge(hi_done, 2 * i + u + 1)
                    pool.tensor_tensor(interior(pad_lo[u]), xn[u][:].rearrange("p (h w) -> p h w", w=W),
                                       interior(pad_hi[u]), ALU.subtract).then_inc(lo_done, 1)

        @block.scalar
        def _(act):
            def high_weights():
                for n, hi in enumerate((wi_hi, ws_hi, wg_hi)):
                    act.wait_ge(prep_T, n + 1)
                    if n == 2:
                        act.copy(wgT[:], wgroup(2)).then_inc(wgt_done, 1)
                    act.activation(hi[:], wgroup(n), ACT.Copy).then_inc(prep_hi, 1)
                act.wait_ge(prep_T, 6)
                act.wait_ge(wc_zero, 3)
                for q in range(Q):
                    act.activation(diagonal(taps33(wc_hi), q), diagonal(wconv_ps, q), ACT.Copy).then_inc(prep_hi, 1)
                for q in range(Q):
                    for e, rows in WT_PARTS:
                        act.activation(wt_block(wt_hi, e, rows, q), wt_source(e, rows, q), ACT.Copy).then_inc(prep_wt, 1)
                act.wait_ge(prep_hi, 3 + Q)
                act.activation(wc_hi[:, 4, :], wconv_ps[:, 1, 1, :], ACT.Copy).then_inc(prep_hi, 1)

            def square_root(g):
                act.wait_ge(gn_step, GN_STEPS * g + 5)
                act.activation(sd[:], var_eps[:], ACT.Sqrt).then_inc(sd_done, 1)

            def chunk0(g):
                square_root(g)
                act.wait_ge(gn_step, GN_STEPS * (g + 1))
                def high_image(j):
                    act.activation(img[:, CH * g + j, :, 0, :], xn0[j][:].rearrange("p (h w) -> p h w", w=W),
                                   ACT.Copy).then_inc(hi0_done, 1)

                for j in range(1, CH):
                    act.wait_ge(lo0_done, (CH - 1) * g + j)
                    act.activation(xn0[j][:], img32[:, CH * g + j].rearrange("p h w -> p (h w)"), ACT.Identity,
                                   bias=nbias[:, j:j + 1], scale=rstd[:, j:j + 1]).then_inc(xn0_done, 1)
                    if j == 1:
                        act.wait_ge(xn0v_done, g + 1)
                    else:
                        act.wait_ge(xn0_done, (CH - 1) * g + j - 1)
                    high_image(j - 1)
                act.wait_ge(xn0_done, (CH - 1) * (g + 1))
                high_image(CH - 1)

            act.wait_ge(warm_set, 1)
            act.activation(warm[:, 2:3], warm[:, 0:1], ACT.Sqrt).then_inc(warmed, 1)
            with act.Fori(0, CHUNKS - 2) as g:
                chunk0(g)
            high_weights()
            for g in range(CHUNKS - 2, CHUNKS):
                chunk0(g)

            def high_z(it, s):
                n = width(s % NB)
                act.wait_ge(z_ready, it + 1)
                act.activation(z_hi[:, 0:n], zbank(s)[:, 0:n], ACT.Identity, scale=z_unscale[:]).then_inc(z_hi_done, 1)

            def item(j, s, last):
                it = 2 * NB * j + s
                n = width(s % NB)
                b0, b1 = BLOCKS[s % NB]
                p = s % 2
                act.wait_ge(h_done, it + 1)
                for m, gt in enumerate(GATE_ORDER):
                    act.wait_ge(gate_ready, GATES * it + m + 1)
                    act.activation(gate[p][m][:, 0:n], gbank(s, m)[:, 0:n],
                                   ACT.Tanh if gt == G_GATE else ACT.Sigmoid,
                                   bias=gate_bias[:, gt:gt + 1]).then_inc(gate_done, 1)
                if not last:
                    high_z(it + 1, s + 1)
                act.wait_ge(c_done, NB + it + 1)
                act.activation(tc[p][:, 0:n], cell[:, W * b0:W * b1], ACT.Tanh).then_inc(tc_done, 1)

            act.activation(warm[:, 1:2], warm[:, 0:1], ACT.Sigmoid).then_inc(warmed, 1)
            high_z(0, 0)
            with act.Fori(0, H // 2 - 1) as j:
                for s in range(2 * NB):
                    item(j, s, False)
            for s in range(2 * NB):
                item(H // 2 - 1, s, s == 2 * NB - 1)

            def high(b, j, free):
                act.wait_ge(xn_done, b + 1)
                if free:
                    act.wait_ge(conv_done, 2 * b - 2)
                act.activation(interior(pad_hi[j % 2]), xn[j % 2][:].rearrange("p (h w) -> p h w", w=W),
                               ACT.Copy).then_inc(hi_done, 1)

            def evacuate(b, j, half_b, s):
                if s == 0:
                    act.wait_ge(stored[j % 2], 16 * half_b)
                act.wait_ge(conv_done, 2 * b + s + 1)
                act.activation(ybuf[j % 2][:, 512 * s:512 * s + 512], ps[:, (2 * j + s) % 4, :], ACT.Identity,
                               bias=conv_bias[:], scale=y_unscale[:]).then_inc(y_done, 1)

            def chunk1(c, first, last):
                for j in range(CH):
                    b = CH * c + j
                    high(b, j, not first or j >= 2)
                    if not first or j >= 2:
                        evacuate(b - 2, (j - 2) % CH, 2 * c + (j - 2) // 2, 1)
                    if j == CH - 1 and not last:
                        square_root(CHUNKS + c + 1)
                    if not first or j >= 1:
                        evacuate(b - 1, (j - 1) % CH, 2 * c + (j - 1) // 2, 0)

            act.wait_ge(pads_zero, PAD_BUFFERS)
            square_root(CHUNKS)
            chunk1(0, True, False)
            with act.Fori(1, CHUNKS - 1) as c:
                chunk1(c, False, False)
            chunk1(CHUNKS - 1, False, True)
            evacuate(B - 2, CH - 2, B // 2 - 1, 1)
            for s in range(2):
                evacuate(B - 1, CH - 1, B // 2 - 1, s)

        @block.tensor
        def _(pe):
            def sum_means(g):
                pe.wait_ge(aggr_done, CH * (g + 1))
                pe.matmul(gn_ps[:, 0:CH], group_mean[:], mv[:, :, 0], start=True, stop=True).then_inc(mean_ready, 1)

            def sum_vars(g):
                pe.wait_ge(gn_step, GN_STEPS * g + 4)
                pe.matmul(gn_ps[:, CH:2 * CH], group_mean[:], vdev[:], start=True, stop=True).then_inc(var_ready, 1)

            pe.wait_ge(par_in, 16 * PARAMETERS)
            for g in range(2):
                sum_means(g)
                sum_vars(g)
            pe.wait_ge(raws_ready, 2 + 1 + 9)
            for k in range(2):
                ins = pe.transpose(wgroup(0)[:, k, :], turn_i[:, k, :], ident[:])
            ins.then_inc(prep_T, 1)
            for k in range(3):
                ins = pe.transpose(wgroup(1)[:, k, :], raw_s[:, :, k], ident[:])
            ins.then_inc(prep_T, 1)
            for k in range(GATES):
                ins = pe.transpose(wgroup(2)[:, k, :], raw_g[:, k, :], ident[:])
            ins.then_inc(prep_T, 1)
            for d in range(3):
                for e in range(3):
                    ins = pe.transpose(wgroup(3 + d)[:, e, :], turn_c[:, 3 * d + e, :], ident[:])
                ins.then_inc(prep_T, 1)
            with pe.Fori(2, CHUNKS - 2) as g:
                sum_means(g)
                sum_vars(g)
            pe.wait_ge(wgt_done, 1)
            pe.wait_ge(bias_ready, 1)
            for k in range(GATES):
                ins = pe.matmul(ps[:, 6, k:k + 1], wgT[:, k, :], bsum[:, 0:1], start=True, stop=True)
            ins.then_inc(prep_T, 1)
            for g in range(CHUNKS - 2, CHUNKS):
                sum_means(g)
                sum_vars(g)

            PASSES_I = ((wi_hi, 0), (wi_lo, 0), (wi_hi, 1))

            def input_conv(t, s, k):
                b0, b1 = BLOCKS[k]
                z = zbank(s)[:, 0:width(k)].rearrange("p (b w) -> p b w", w=W)
                for m, (w, half) in enumerate(PASSES_I):
                    pe.matmul(z, w[:, 1, :], img[:, b0:b1, t, half, :], start=(m == 0), stop=False)
                    pe.matmul(z[:, :, 1:W], w[:, 0, :], img[:, b0:b1, t, half, 0:W - 1], start=False, stop=False)

            def item(j, s, last):
                u, k = s // NB, s % NB
                it = 2 * NB * j + s
                b0, b1 = BLOCKS[k]
                n = width(k)
                z = zbank(s)[:, 0:n]
                pe.wait_ge(hh_done, NB * (2 * j + u) + min(k + 2, NB))
                for w in (ws_hi, ws_lo):
                    for tap in range(3):
                        pe.matmul(z, w[:, tap, :], hh[1 - u][:, W * b0 + tap:W * b1 + tap], start=False, stop=False)
                pe.wait_ge(hl_done, NB * (2 * j + u) + min(k + 2, NB))
                for tap in range(3):
                    ins = pe.matmul(z, ws_hi[:, tap, :], hl[1 - u][:, W * b0 + tap:W * b1 + tap],
                                    start=False, stop=(tap == 2))
                ins.then_inc(z_ready, 1)
                if not last:
                    pe.wait_ge(z_lo_done, it + 1)
                    input_conv(2 * j + (s + 1) // NB, s + 1, (k + 1) % NB)
                pe.wait_ge(z_hi_done, it + 1)
                for m in range(2):
                    pe.wait_ge(gate_done, GATES * it + m + 1)
                    pe.matmul(gbank(s, m)[:, 0:n], wg_hi[:, GATE_ORDER[m], :], z_hi[:, 0:n], start=True, stop=False)
                    pe.matmul(gbank(s, m)[:, 0:n], wg_lo[:, GATE_ORDER[m], :], z_hi[:, 0:n], start=False, stop=False)
                pe.wait_ge(z_lo_done, Z_AHEAD + it + 1)
                for m in range(2):
                    pe.matmul(gbank(s, m)[:, 0:n], wg_hi[:, GATE_ORDER[m], :], z_lo[:, 0:n],
                              start=False, stop=True).then_inc(gate_ready, 1)
                for m in range(2, GATES):
                    pe.wait_ge(gate_done, GATES * it + m + 1)
                    pe.matmul(gbank(s, m)[:, 0:n], wg_hi[:, GATE_ORDER[m], :], z_hi[:, 0:n], start=True, stop=False)
                    pe.matmul(gbank(s, m)[:, 0:n], wg_lo[:, GATE_ORDER[m], :], z_hi[:, 0:n], start=False, stop=False)
                    pe.matmul(gbank(s, m)[:, 0:n], wg_hi[:, GATE_ORDER[m], :], z_lo[:, 0:n],
                              start=False, stop=True).then_inc(gate_ready, 1)

            pe.wait_ge(lo0_done, (CH - 1) * (CHUNKS + 1))
            pe.wait_ge(lo0v_done, CHUNKS)
            input_conv(0, 0, 0)
            pe.wait_ge(hh_done, NB)
            pe.wait_ge(hl_done, NB)
            with pe.Fori(0, H // 2 - 1) as j:
                for s in range(2 * NB):
                    item(j, s, False)
            for s in range(2 * NB):
                item(H // 2 - 1, s, s == 2 * NB - 1)

            TAPS = [(d, e) for d in range(3) for e in range(3)]
            DENSE = ([(wc_hi[:, 4, :], pad_hi, 1, 1), (wc_lo[:], pad_hi, 1, 1)]
                     + [(wc_hi[:, 3 * d + e, :], pad_lo, d, e) for d, e in TAPS])

            def bank(j, s):
                return ps[:, (2 * j + s) % 4, :].rearrange("p (h w) -> p h w", w=W)

            def dense_half(b, j, s, free):
                if free:
                    pe.wait_ge(y_done, 2 * b + s - 3)
                for m, (w, t, d, e) in enumerate(DENSE):
                    pe.matmul(bank(j, s), w, padded(t[j % 2], s, d - 1, e - 1), start=(m == 0), stop=False,
                              skip_group_check=True)

            def tiled_half(j, s):
                for w in (wt_hi, wt_lo):
                    for d in range(3):
                        for q in range(Q):
                            last = w is wt_lo and d == 2
                            r = slice(32 * q, 32 * q + 32)
                            ins = pe.matmul(bank(j, s)[r], w[:, d, q, :],
                                            padded(shifted[j % 2][:, q, :], s, d - 1, 0), start=False, stop=last,
                                            tile_position=(0, 32 * q), skip_group_check=True)
                ins.then_inc(conv_done, 1)

            def chunk1(c, first, last):
                for j in range(CH):
                    b = CH * c + j
                    pe.wait_ge(lo_done, b + 1)
                    dense_half(b, j, 0, not first or j >= 2)
                    dense_half(b, j, 1, not first or j >= 2)
                    pe.wait_ge(shifted_in[j % 2], 16 * 2 * Q * (2 * c + j // 2 + 1))
                    pe.wait_ge(unshifted_done, Q * (b + 1))
                    tiled_half(j, 0)
                    tiled_half(j, 1)
                    if not last:
                        if j == 0:
                            sum_means(CHUNKS + c + 1)
                        if j == 1:
                            sum_vars(CHUNKS + c + 1)

            pe.wait_ge(pads_zero, PAD_BUFFERS)
            sum_means(CHUNKS)
            sum_vars(CHUNKS)
            chunk1(0, True, False)
            with pe.Fori(1, CHUNKS - 1) as c:
                chunk1(c, False, False)
            chunk1(CHUNKS - 1, False, True)


_INS = ["x", "L0_conv_w_i2s", "L0_conv_b_i2s", "L0_conv_w_s2s", "L0_conv_b_s2s", "L0_conv_w_ih", "L0_conv_b_ih",
        "L0_conv_b_hh", "L1_conv_W", "L1_conv_b"]


def shape_constants():
    c = np.arange(P)
    same_group = (c[:, None] % 32 == c[None, :] % 32).astype(np.float32) / Q
    kept = (c[:, None] % 3 >= c[None, :] % 3).astype(np.float32)
    return np.stack([np.eye(P, dtype=np.float32), same_group, kept])


def kernel(**inputs):
    import concourse.bacc as _bacc
    from concourse.bass_utils import run_bass_kernel_spmd as _run

    nc = _bacc.Bacc("TRN2", target_bir_lowering=False, num_devices=1)
    arrays, args = {}, []
    for name in _INS:
        a = np.ascontiguousarray(inputs[name])
        arrays[f"in_{name}_dram"] = a
        args.append(nc.dram_tensor(f"in_{name}_dram", a.shape, mybir.dt.from_np(a.dtype), kind="ExternalInput").ap())
    arrays["in_consts_dram"] = shape_constants()
    args.append(nc.dram_tensor("in_consts_dram", (3, P, P), F32, kind="ExternalInput").ap())
    out = nc.dram_tensor("out_0_dram", (B, P, H, W), F32, kind="ExternalOutput").ap()
    build_network(nc, *args, out)
    r = _run(nc, [arrays], core_ids=[0])
    return r.results[0]["out_0_dram"]
```

```python
from contextlib import ExitStack

import numpy as np
import concourse.bass as bass
from concourse import mybir

F32 = mybir.dt.float32
F32R = mybir.dt.float32r
F16 = mybir.dt.float16
I32 = mybir.dt.int32
ALU = mybir.AluOpType
ACT = mybir.ActivationFunctionType
AX = mybir.AxisListType

P = 128
B, H, W = 32, 32, 32
HW = H * W
Q = 4
GATES = 4

ACT_SCALE = 512.0
WEIGHT_TOP = 4096.0
EXPONENT_BITS = 0x7F800000

BLOCKS = [(0, 11), (11, 21), (21, 32)]
NB = len(BLOCKS)
ITEMS = NB * H
F_GATE, I_GATE, G_GATE, O_GATE = 1, 0, 2, 3
GATE_ORDER = [F_GATE, I_GATE, G_GATE, O_GATE]
GATE_BANKS = 6

CH = 4
CHUNKS = B // CH
GN_STEPS = 10

H_AHEAD = 2
LO0_DONE = CH * CHUNKS + CH // 2
PARAMETERS = 11
Z_AHEAD = 1
ROW_AHEAD = 2
BLOCK_COPIES = 2 * (1 + 3 * Q)


def width(k):
    return W * (BLOCKS[k][1] - BLOCKS[k][0])


PADW = W + 1
PADN = 1 + (H + 2) * PADW + 1


def build_network(nc, x, w_i2s, b_i2s, w_s2s, b_s2s, w_ih, b_ih, b_hh, w_conv, b_conv, consts, out):
    x_q = x.rearrange("b (n q) h w -> q n b (h w)", q=Q)
    out_q = out.rearrange("b (n q) h w -> q n b (h w)", q=Q)

    with ExitStack() as ctx:
        def sb(name, shape, dt, stack=ctx):
            return stack.enter_context(nc.sbuf_tensor(name, shape, dt))

        def sem(name):
            return ctx.enter_context(nc.semaphore(name))

        img = sb("img", [P, B, H, 2, W], F16)
        img32 = img[:].rearrange("p b h s w -> p (b h s w)").bitcast(F32).rearrange("p (b h w) -> p b h w", b=B, h=H)
        group_mean = sb("group_mean", [P, P], F32)
        wc_hi = sb("wc_hi", [P, P], F16)
        wc_lo = sb("wc_lo", [P, P], F16)
        wt_hi = sb("wt_hi", [P, 3, Q, 32], F16)
        wt_lo = sb("wt_lo", [P, 3, Q, 32], F16)
        z_unscale = sb("z_unscale", [P, 1], F32)
        y_unscale = sb("y_unscale", [P, 1], F32)
        gate_bias = sb("gate_bias", [P, GATES], F32)
        conv_bias = sb("conv_bias", [P, 1], F32)
        bn = sb("bn", [P, CH, 2, 6], F32)
        mv = sb("mv", [P, CH, 2], F32)
        gmean = sb("gmean", [P, CH], F32)
        dev = sb("dev", [P, CH], F32)
        dev2 = sb("dev2", [P, CH], F32)
        vdev = sb("vdev", [P, CH], F32)
        warm = sb("warm", [P, 4], F32)
        var_eps = sb("var_eps", [P, CH], F32)
        sd = sb("sd", [P, CH], F32)
        rs0 = sb("rs0", [P, CH], F32)
        newton = [sb(f"newton{i}", [P, CH], F32) for i in range(2)]
        brow = sb("brow", [P, 2 + 2 * GATES], F32)
        bsum = sb("bsum", [P, 1 + GATES], F32)
        top = sb("top", [P, 8], F32)
        scl = sb("scl", [P, 6], F32)
        rstd = sb("rstd", [P, CH], F32)
        nbias = sb("nbias", [P, CH], F32)

        with ExitStack() as s01:
            wi_hi = sb("wi_hi", [P, 2, P], F16, s01)
            wi_lo = sb("wi_lo", [P, 2, P], F16, s01)
            ws_hi = sb("ws_hi", [P, 3, P], F16, s01)
            ws_lo = sb("ws_lo", [P, 3, P], F16, s01)
            wg_hi = sb("wg_hi", [P, GATES, P], F32R, s01)
            wg_lo = sb("wg_lo", [P, GATES, P], F32R, s01)
            wall_hi = sb("wall_hi", [P, 3, 3, P], F16, s01)
            wall_lo = sb("wall_lo", [P, 3, 3, P], F16, s01)
            wgT = sb("wgT", [P, GATES, P], F32, s01)
            with ExitStack() as s0:
                xn0 = [sb(f"xn0{i}", [P, HW], F32, s0) for i in range(CH)]
                ident = sb("ident", [P, P], F32, s0)
                raw_i = sb("raw_i", [P, P, 3], F32, s0)
                raw_s = sb("raw_s", [P, P, 3], F32, s0)
                raw_g = sb("raw_g", [P, GATES, P], F32, s0)
                raw_c = sb("raw_c", [P, P, 9], F32, s0)
                turn_i = sb("turn_i", [P, 2, P], F32, s0)
                turn_c = sb("turn_c", [P, 9, P], F32, s0)
                raw_cb = sb("raw_cb", [P, P], F32, s0)
                mask = sb("mask", [P, P], F32, s0)
            with ExitStack() as s1:
                gate = [[sb(f"gate{i}{j}", [P, 352], F32, s1) for j in range(GATES)] for i in range(2)]
                fc = [sb(f"fc{i}", [P, 352], F32, s1) for i in range(2)]
                ig = [sb(f"ig{i}", [P, 352], F32, s1) for i in range(2)]
                hT = [sb(f"hT{i}", [P, 352], F32, s1) for i in range(2)]
                tc = [sb(f"tc{i}", [P, 352], F32, s1) for i in range(2)]
                z_hi = sb("z_hi", [P, 352], F32R, s1)
                z_lo = sb("z_lo", [P, 352], F32R, s1)
                hrow = [sb(f"hrow{i}", [P, B * W], F32, s1) for i in range(2)]
                hh = [sb(f"hh{i}", [P, B * W + 2], F16, s1) for i in range(2)]
                hl = [sb(f"hl{i}", [P, B * W + 2], F16, s1) for i in range(2)]
                cell = sb("cell", [P, B * W], F32, s1)
        with ExitStack() as s2:
            xn = [sb(f"xn{i}", [P, HW], F32, s2) for i in range(2)]
            pad = [sb(f"pad{i}", [P, 2, PADN], F16, s2) for i in range(2)]
            shifted = [sb(f"shifted{i}", [P, Q, 2, PADN], F16, s2) for i in range(2)]
            ybuf = [sb(f"ybuf{i}", [P, HW], F32, s2) for i in range(2)]
            xs = [sb(f"xs{i}", [P, HW], F32, s2) for i in range(CH)]

        ps = ctx.enter_context(nc.psum_tensor("ps", [P, 8, 512], F32))

        group_in = sem("group_in")
        par_in = sem("par_in")
        x_in = [[sem(f"x_in{i}{j}") for j in range(CH)] for i in range(2)]
        prep = sem("prep")
        scales_ready = sem("scales_ready")
        raws_ready = sem("raws_ready")
        bias_ready = sem("bias_ready")
        prep_T = sem("prep_T")
        wgt_done = sem("wgt_done")
        prep_hi = sem("prep_hi")
        wall_hi_done = sem("wall_hi_done")
        split_done = sem("split_done")
        gate_bias_done = sem("gate_bias_done")
        blocks_in = sem("blocks_in")
        warm_set = sem("warm_set")
        warmed = sem("warmed")
        waited = sem("waited")
        bn_done = sem("bn_done")
        aggr_done = sem("aggr_done")
        mean_ready = sem("mean_ready")
        var_ready = sem("var_ready")
        gn_step = sem("gn_step")
        sd_done = sem("sd_done")
        xn0_done = sem("xn0_done")
        xn0v_done = sem("xn0v_done")
        hi0_done = sem("hi0_done")
        lo0_done = sem("lo0_done")
        lo0v_done = sem("lo0v_done")
        z_ready = sem("z_ready")
        z_hi_done = sem("z_hi_done")
        z_lo_done = sem("z_lo_done")
        gate_ready = sem("gate_ready")
        gate_done = sem("gate_done")
        fc_done = sem("fc_done")
        ig_done = sem("ig_done")
        c_done = sem("c_done")
        tc_done = sem("tc_done")
        h_done = sem("h_done")
        hh_done = sem("hh_done")
        hl_done = sem("hl_done")
        wt_zero = sem("wt_zero")
        ht_done = sem("ht_done")
        row_done = sem("row_done")
        xs_in = [sem(f"xs_in{i}") for i in range(CH)]
        h_upper = sem("h_upper")
        x1_upper = sem("x1_upper")
        x1_done = sem("x1_done")
        pads_zero = sem("pads_zero")
        shifted_in = [sem(f"shifted_in{i}") for i in range(2)]
        unshifted_done = sem("unshifted_done")
        last_shift_done = sem("last_shift_done")
        xn_done = sem("xn_done")
        pads_used = sem("pads_used")
        hi_done = sem("hi_done")
        lo_done = sem("lo_done")
        conv_done = sem("conv_done")
        y_done = sem("y_done")
        last_sum_done = sem("last_sum_done")
        sum_done = sem("sum_done")
        stored = [sem(f"stored{i}") for i in range(2)]

        block = ctx.enter_context(nc.Block())

        def zbank(it):
            return ps[:, it % 2, :]

        def gbank(it, n):
            return ps[:, 2 + (GATES * it + n) % GATE_BANKS, :]

        gn_ps = ps[:, 7, 0:2 * CH]

        def padded(t, half, dh, dw):
            at = 1 + (16 * half + 1 + dh) * PADW + dw
            return t[:, at:at + 16 * PADW].rearrange("p (h w) -> p h w", w=PADW)[:, :, 0:W]

        def flat(t):
            return t.rearrange("p a b -> p (a b)")

        SHIFTS = [(e, q) for e in (0, 2) for q in range(Q)]

        def shift_to(slot, e, q):
            return flat(shifted[slot][32 * e:32 * e + 32, q])[:, 1:2 * PADN - 1]

        def shift_from(slot, e, q):
            return flat(pad[slot][32 * q:32 * q + 32])[:, e:e + 2 * PADN - 2]

        def interior(t, part):
            return t[:, part, 1 + PADW:1 + PADW + H * PADW].rearrange("p (h w) -> p h w", w=PADW)[:, :, 0:W]

        def wgroup(n):
            return ps[:, n, 0:[2, 3, 4][n] * P].rearrange("p (a b) -> p a b", b=P)

        wconv_ps = ps[:, 3:6, 0:3 * P].rearrange("p d (e o) -> p d e o", o=P)

        WT_PARTS = ((0, slice(0, 3)), (1, slice(0, 3, 2)), (2, slice(0, 3)))

        def wt_block(t, e, rows, q):
            return t[32 * e:32 * e + 32, rows, q, :]

        def wt_source(t, e, rows, q):
            return t[32 * q:32 * q + 32, rows, e, 32 * q:32 * q + 32]

        @block.sync
        def _(sp):
            def load_x(g, j):
                b = CH * g + j
                sp.dma_start(img32[:, b].rearrange("p h w -> p (h w)"), x_q[:, :, b, :]).then_inc(x_in[g % 2][j], 16)

            for g in range(3):
                for j in range(CH):
                    if g > 1:
                        sp.wait_ge(x_in[g % 2][j], 16 * (g // 2))
                    load_x(g, j)
                if g == 0:
                    sp.dma_start(group_mean[:], consts[1]).then_inc(group_in, 16)
            sp.dma_start(raw_i[:], w_i2s.rearrange("o i a k -> o i (a k)")).then_inc(par_in, 16)
            sp.dma_start(raw_s[:], w_s2s.rearrange("o i a k -> o i (a k)")).then_inc(par_in, 16)
            sp.dma_start(raw_g[:], w_ih.rearrange("(j p) s -> p j s", p=P)).then_inc(par_in, 16)
            for n, t in ((0, ident), (2, mask)):
                sp.dma_start(t[:], consts[n]).then_inc(par_in, 16)
            with nc.allow_non_contiguous_dma(reason="bias columns"):
                sp.dma_start(brow[:, 0:1], b_i2s.rearrange("(p a) -> p a", a=1)).then_inc(par_in, 16)
                sp.dma_start(brow[:, 1:2], b_s2s.rearrange("(p a) -> p a", a=1)).then_inc(par_in, 16)
                sp.dma_start(brow[:, 2:2 + GATES], b_ih.rearrange("(j p) -> p j", p=P)).then_inc(par_in, 16)
                sp.dma_start(brow[:, 2 + GATES:2 + 2 * GATES], b_hh.rearrange("(j p) -> p j", p=P)).then_inc(par_in, 16)
            sp.dma_start(raw_c[:].rearrange("p i k -> p (i k)"), w_conv.rearrange("(n q) i a k -> q n (i a k)", q=Q)).then_inc(par_in, 16)
            sp.dma_start(raw_cb[:], b_conv.rearrange("(n q) i -> q n i", q=Q)).then_inc(par_in, 16)
            for g in range(3, CHUNKS):
                for j in range(CH):
                    sp.wait_ge(x_in[g % 2][j], 16 * (g // 2))
                    load_x(g, j)

            def place_blocks():
                sp.wait_ge(split_done, 4)
                sp.wait_ge(wt_zero, 2)
                for t, centre, src in ((wt_hi, wc_hi, wall_hi), (wt_lo, wc_lo, wall_lo)):
                    sp.dma_start(centre[:], src[:, 1, 1, :]).then_inc(blocks_in, 16)
                    for q in range(Q):
                        for e, rows in WT_PARTS:
                            sp.dma_start(wt_block(t, e, rows, q), wt_source(src, e, rows, q)).then_inc(blocks_in, 16)

            def shift(b, slot, free):
                sp.wait_ge(lo_done, b + 1)
                if free:
                    sp.wait_ge(conv_done, 2 * b - 2)
                for e, q in SHIFTS[:-1]:
                    sp.dma_start(shift_to(slot, e, q), shift_from(slot, e, q)).then_inc(shifted_in[slot], 16)

            def store(b, slot):
                sp.wait_ge(sum_done, b + 1)
                sp.dma_start(out_q[:, :, b, :], ybuf[slot][:]).then_inc(stored[slot], 16)

            def load_xs(b, slot):
                sp.dma_start(xs[slot][:], x_q[:, :, b, :]).then_inc(xs_in[slot], 16)

            def chunk1(c, first, ahead):
                for j in range(CH):
                    shift(CH * c + j, j % 2, not first or j >= 2)
                    if ahead:
                        sp.wait_ge(x1_done, CH * (c + 1) + j + 1)
                        load_xs(CH * (c + 2) + j, j)
                    if not first or j >= 2:
                        store(CH * c + j - 2, j % 2)

            for j in range(CH):
                load_xs(j, j)
            place_blocks()
            for j in range(CH):
                sp.wait_ge(x1_done, j + 1)
                load_xs(CH + j, j)
            sp.wait_ge(pads_zero, 3)
            chunk1(0, True, True)
            with sp.Fori(1, CHUNKS - 2) as c:
                chunk1(c, False, True)
            for c in range(CHUNKS - 2, CHUNKS):
                chunk1(c, False, False)
            store(B - 2, 0)
            for s in range(2):
                half = slice(HW // 2 * s, HW // 2 * (s + 1))
                sp.wait_ge(last_sum_done, s + 1)
                sp.dma_start(out_q[:, :, B - 1, half], ybuf[1][:, half]).then_inc(stored[1], 16)
            sp.wait_ge(stored[0], 16 * (B // 2))
            sp.wait_ge(stored[1], 16 * (B // 2 + 1))

        @block.vector
        def _(v):
            n_prep = [0]

            def step(ins):
                n_prep[0] += 1
                ins.then_inc(prep, 1)

            def settle():
                v.wait_ge(prep, n_prep[0])

            def image(b):
                return img32[:, b].rearrange("p h w -> p (h w)")

            def apart():
                v.sem_inc(waited, 1)

            def bn_stats(src, j):
                for s in range(2):
                    v.bn_stats(bn[:, j, s, :], src[:, 512 * s:512 * s + 512]).then_inc(bn_done, 1)

            def bn_aggr(g):
                v.wait_ge(bn_done, 2 * CH * (g + 1))
                apart()
                for j in range(CH):
                    v.bn_aggr(mv[:, j, :], bn[:, j, :, :].rearrange("p a b -> p (a b)")).then_inc(aggr_done, 1)

            def gn_wait(g, k):
                v.wait_ge(gn_step, GN_STEPS * g + k)

            def chain_mean(g):
                v.wait_ge(mean_ready, g + 1)
                v.tensor_copy(gmean[:], gn_ps[:, 0:CH]).then_inc(gn_step, 1)
                v.tensor_tensor(dev[:], mv[:, :, 0], gn_ps[:, 0:CH], ALU.subtract).then_inc(gn_step, 1)
                gn_wait(g, 2)
                v.tensor_tensor(dev2[:], dev[:], dev[:], ALU.mult).then_inc(gn_step, 1)
                gn_wait(g, 3)
                v.tensor_tensor(vdev[:], dev2[:], mv[:, :, 1], ALU.add).then_inc(gn_step, 1)

            def chain_var(g):
                v.wait_ge(var_ready, g + 1)
                v.tensor_scalar(var_eps[:], gn_ps[:, CH:2 * CH], 1e-5, None, ALU.add).then_inc(gn_step, 1)

            def chain_rstd(g):
                v.wait_ge(sd_done, g + 1)
                v.reciprocal(rs0[:], sd[:]).then_inc(gn_step, 1)
                gn_wait(g, 6)
                v.tensor_tensor(newton[0][:], rs0[:], rs0[:], ALU.mult).then_inc(gn_step, 1)
                gn_wait(g, 7)
                v.scalar_tensor_tensor(out=newton[1][:], in0=newton[0][:], scalar=-0.5 / ACT_SCALE ** 2, in1=var_eps[:],
                                       op0=ALU.mult, op1=ALU.mult).then_inc(gn_step, 1)
                gn_wait(g, 8)
                v.scalar_tensor_tensor(out=rstd[:], in0=newton[1][:], scalar=1.5, in1=rs0[:],
                                       op0=ALU.add, op1=ALU.mult).then_inc(gn_step, 1)
                gn_wait(g, 9)
                v.scalar_tensor_tensor(out=nbias[:], in0=gmean[:], scalar=-1.0, in1=rstd[:],
                                       op0=ALU.mult, op1=ALU.mult).then_inc(gn_step, 1)

            v.memset(hh[0][:], 0.0).then_inc(hh_done, NB - 1)
            v.memset(hh[1][:], 0.0).then_inc(hh_done, 1)
            v.memset(hl[0][:], 0.0).then_inc(hl_done, NB - 1)
            v.memset(hl[1][:], 0.0).then_inc(hl_done, 1)
            v.memset(cell[:], 0.0).then_inc(c_done, NB)
            for j in range(CH):
                v.wait_ge(x_in[0][j], 16)
                bn_stats(image(j), j)
            bn_aggr(0)

            def scale_weights():
                v.wait_ge(par_in, 16 * PARAMETERS)
                step(v.tensor_tensor(raw_i[:, :, 1], raw_i[:, :, 1], mask[:], ALU.mult))
                settle()
                step(v.tensor_reduce(top[:, 0:1], raw_i[:, :, 0:2], AX.XY, ALU.max, apply_absolute_value=True))
                step(v.tensor_reduce(top[:, 1:2], raw_s[:], AX.XY, ALU.max, apply_absolute_value=True))
                step(v.tensor_reduce(top[:, 2:3], raw_c[:, :, 4], AX.X, ALU.max, apply_absolute_value=True))
                for q in range(Q):
                    r = slice(32 * q, 32 * q + 32)
                    step(v.tensor_reduce(top[r, 3:4], raw_c[r].rearrange("p (n q) k -> p q n k", q=Q)[:, q], AX.XY,
                                         ALU.max, apply_absolute_value=True))
                step(v.tensor_reduce(conv_bias[:], raw_cb[:], AX.X, ALU.add))
                v.tensor_tensor(bsum[:, 0:1], brow[:, 0:1], brow[:, 1:2], ALU.add).then_inc(bias_ready, 1)
                step(v.tensor_tensor(bsum[:, 1:1 + GATES], brow[:, 2:2 + GATES], brow[:, 2 + GATES:2 + 2 * GATES], ALU.add))
                settle()
                step(v.tensor_tensor(top[:, 4:5], top[:, 0:1], top[:, 1:2], ALU.max))
                step(v.tensor_tensor(top[:, 5:6], top[:, 2:3], top[:, 3:4], ALU.max))
                settle()
                step(v.tensor_scalar(top[:, 6:8], top[:, 4:6], 2.0 ** -90, None, ALU.max))
                settle()
                step(v.tensor_scalar(scl[:, 0:2].bitcast(I32), top[:, 6:8].bitcast(I32), EXPONENT_BITS, None, ALU.bitwise_and))
                settle()
                step(v.reciprocal(scl[:, 2:4], scl[:, 0:2]))
                step(v.tensor_scalar(z_unscale[:], scl[:, 0:1], 1.0 / (WEIGHT_TOP * ACT_SCALE), None, ALU.mult))
                step(v.tensor_scalar(y_unscale[:], scl[:, 1:2], 1.0 / (WEIGHT_TOP * ACT_SCALE), None, ALU.mult))
                settle()
                v.tensor_scalar(scl[:, 4:6], scl[:, 2:4], WEIGHT_TOP, None, ALU.mult).then_inc(scales_ready, 1)

            def split_weights():
                v.wait_ge(prep_T, 6)
                v.tensor_copy(wgT[:], wgroup(2)).then_inc(wgt_done, 1)
                for n, (hi, lo) in enumerate(((wi_hi, wi_lo), (ws_hi, ws_lo), (wg_hi, wg_lo))):
                    v.tensor_copy(hi[:], wgroup(n)).then_inc(prep_hi, 1)
                for n, (hi, lo) in enumerate(((wi_hi, wi_lo), (ws_hi, ws_lo), (wg_hi, wg_lo))):
                    v.wait_ge(prep_hi, n + 1)
                    high = hi[:].bitcast(F32) if n == 2 else hi[:]
                    v.tensor_tensor(lo[:], wgroup(n), high, ALU.subtract).then_inc(split_done, 1)
                v.wait_ge(prep_T, 7)
                v.tensor_tensor(gate_bias[:], ps[:, 6, 0:GATES], bsum[:, 1:1 + GATES], ALU.add).then_inc(gate_bias_done, 1)

            def low_conv_weights():
                v.wait_ge(wall_hi_done, 1)
                v.tensor_tensor(wall_lo[:], wconv_ps, wall_hi[:], ALU.subtract).then_inc(split_done, 1)

            def norm_image(g, j):
                v.wait_ge(lo0_done, CH * g + j + 1)
                v.tensor_scalar(xn0[j][:], image(CH * g + j), gmean[:, j:j + 1], rstd[:, j:j + 1],
                                ALU.subtract, ALU.mult).then_inc(xn0v_done, 1)

            def chunk0(i, u, last):
                g = 2 * i + u
                chain_mean(g)
                for j in range(CH):
                    if not last:
                        v.wait_ge(x_in[1 - u][j], 16 * (i + 1 + u))
                        apart()
                        bn_stats(image(CH * (g + 1) + j), j)
                    if j == 0:
                        chain_var(g)
                    if j == 1:
                        chain_rstd(g)
                        norm_image(g, 0)
                        if last:
                            norm_image(g, 1)
                if not last:
                    bn_aggr(g + 1)

            chunk0(0, 0, False)
            chunk0(0, 1, False)
            scale_weights()
            with v.Fori(1, CHUNKS // 2 - 1) as i:
                chunk0(i, 0, False)
                chunk0(i, 1, False)
            chunk0(CHUNKS // 2 - 1, 0, False)
            chunk0(CHUNKS // 2 - 1, 1, True)
            split_weights()
            for j in range(CH // 2, CH):
                b = B - CH + j
                v.wait_ge(hi0_done, b + 1)
                v.tensor_tensor(img[:, b, :, 1, :], xn0[j][:].rearrange("p (h w) -> p h w", w=W),
                                img[:, b, :, 0, :], ALU.subtract).then_inc(lo0v_done, 1)
            low_conv_weights()

            v.wait_ge(lo0_done, LO0_DONE)
            v.wait_ge(lo0v_done, CH // 2)

            def zlow(it, s, k):
                n = width(k)
                v.wait_ge(z_hi_done, it + 1)
                v.scalar_tensor_tensor(out=z_lo[:, 0:n], in0=zbank(s)[:, 0:n], scalar=z_unscale[:],
                                       in1=z_hi[:, 0:n].bitcast(F32), op0=ALU.mult,
                                       op1=ALU.subtract).then_inc(z_lo_done, 1)

            def item(j, s, last, final_step):
                u, k = s // NB, s % NB
                it = 2 * NB * j + s
                n = width(k)
                b0, b1 = BLOCKS[k]
                cols = slice(W * b0, W * b1)
                pads = slice(1 + W * b0, 1 + W * b1)
                p = s % 2
                v.wait_ge(gate_done, GATE_BANKS + GATES * it + 3)
                v.tensor_tensor(ig[p][:, 0:n], gate[p][1][:, 0:n], gate[p][2][:, 0:n], ALU.mult).then_inc(ig_done, 1)
                v.wait_ge(ig_done, it + 1)
                v.wait_ge(fc_done, it + 1)
                v.tensor_tensor(cell[:, cols], fc[p][:, 0:n], ig[p][:, 0:n], ALU.add).then_inc(c_done, 1)
                if not last:
                    zlow(it + 1, s + 1, (k + 1) % NB)
                v.wait_ge(tc_done, it + 1)
                v.scalar_tensor_tensor(out=hrow[u][:, cols], in0=gate[p][3][:, 0:n], scalar=ACT_SCALE,
                                       in1=tc[p][:, 0:n], op0=ALU.mult, op1=ALU.mult).then_inc(h_done, 1)
                v.wait_ge(h_done, H_AHEAD + it + 1)
                if not final_step:
                    v.tensor_copy(hh[u][:, pads], hrow[u][:, cols]).then_inc(hh_done, 1)
                    v.wait_ge(hh_done, NB + it + 1)
                    v.tensor_tensor(hl[u][:, pads], hrow[u][:, cols], hh[u][:, pads], ALU.subtract).then_inc(hl_done, 1)
                v.wait_ge(row_done, it + 1)
                v.transpose(hT[p][:, 0:n], hrow[u][:, cols]).then_inc(ht_done, 1)

            zlow(0, 0, 0)
            with v.Fori(0, H // 2 - 1) as j:
                for s in range(2 * NB):
                    item(j, s, False, False)
            for s in range(2 * NB - 1):
                item(H // 2 - 1, s, False, s >= NB)
                if s >= 2:
                    v.wait_ge(x1_upper, s - 1)
                    v.bn_stats(bn[:, s - 2, 0, :], image(s - 2)[:, 0:HW // 2]).then_inc(bn_done, 1)

            def residual(c, j):
                b = CH * c + j
                v.wait_ge(xs_in[j], 16 * (c + 1))
                v.scalar_tensor_tensor(out=image(b), in0=image(b), scalar=1.0 / ACT_SCALE, in1=xs[j][:],
                                       op0=ALU.mult, op1=ALU.add).then_inc(x1_done, 1)
                v.wait_ge(x1_done, b + 1)
                apart()
                bn_stats(image(b), j)

            def unshifted(b, j, free):
                v.wait_ge(lo_done, b + 1)
                if free:
                    v.wait_ge(conv_done, 2 * b - 2)
                for q in range(Q):
                    v.tensor_copy(flat(shifted[j % 2][32:64, q]),
                                  flat(pad[j % 2][32 * q:32 * q + 32])).then_inc(unshifted_done, 1)

            def chunk1(c, first, left):
                last = left == 0
                g = CHUNKS + c
                for j in range(CH):
                    unshifted(CH * c + j, j, not first or j >= 2)
                    if not last:
                        if j == 0:
                            residual(c + 1, 1)
                            residual(c + 1, 2)
                        if j == 1:
                            residual(c + 1, 3)
                            bn_aggr(g + 1)
                        if j == 2:
                            chain_mean(g + 1)
                            chain_var(g + 1)
                            v.wait_ge(xn_done, CH * (c + 1))
                            chain_rstd(g + 1)
                        if j == 3 and left > 1:
                            residual(c + 2, 0)

            def lower_residual(b):
                v.wait_ge(xs_in[b], 16)
                lower = slice(HW // 2, HW)
                v.scalar_tensor_tensor(out=image(b)[:, lower], in0=image(b)[:, lower], scalar=1.0 / ACT_SCALE,
                                       in1=xs[b][:, lower], op0=ALU.mult, op1=ALU.add).then_inc(x1_done, 1)
                v.wait_ge(x1_done, b + 1)
                v.bn_stats(bn[:, b, 1, :], image(b)[:, lower]).then_inc(bn_done, 1)

            v.wait_ge(row_done, ROW_AHEAD + ITEMS - 2)
            lower_residual(0)
            v.wait_ge(x1_upper, CH)
            v.bn_stats(bn[:, CH - 1, 0, :], image(CH - 1)[:, 0:HW // 2]).then_inc(bn_done, 1)
            item(H // 2 - 1, 2 * NB - 1, True, True)
            for b in range(1, CH):
                lower_residual(b)
            bn_aggr(CHUNKS)
            chain_mean(CHUNKS)
            chain_var(CHUNKS)
            chain_rstd(CHUNKS)
            v.wait_ge(row_done, ROW_AHEAD + ITEMS)
            residual(1, 0)
            chunk1(0, True, CHUNKS - 1)
            with v.Fori(1, CHUNKS - 2) as c:
                chunk1(c, False, 2)
            chunk1(CHUNKS - 2, False, 1)
            chunk1(CHUNKS - 1, False, 0)
            for s in range(2):
                half = slice(HW // 2 * s, HW // 2 * (s + 1))
                v.wait_ge(y_done, 2 * (B - 1) + s + 1)
                v.tensor_tensor(ybuf[1][:, half], ybuf[1][:, half], image(B - 1)[:, half], ALU.add).then_inc(last_sum_done, 1)
        @block.gpsimd
        def _(pool):
            pool.memset(warm[:], 1.0).then_inc(warm_set, 1)
            for t in (wt_hi, wt_lo):
                pool.memset(t[:], 0.0).then_inc(wt_zero, 1)
            pool.sem_inc(gate_done, GATE_BANKS)
            pool.sem_inc(h_done, H_AHEAD)
            pool.sem_inc(z_lo_done, Z_AHEAD)
            pool.sem_inc(row_done, ROW_AHEAD)
            pool.sem_inc(lo0_done, CH)

            def low_image(b, j):
                pool.wait_ge(hi0_done, b + 1)
                pool.tensor_tensor(img[:, b, :, 1, :], xn0[j][:].rearrange("p (h w) -> p h w", w=W),
                                   img[:, b, :, 0, :], ALU.subtract).then_inc(lo0_done, 1)

            with pool.Fori(0, CHUNKS - 1) as g:
                for j in range(CH):
                    low_image(CH * g + j, j)
            for j in range(CH // 2):
                low_image(B - CH + j, j)

            def forget(j, s):
                it = 2 * NB * j + s
                n = width(s % NB)
                b0, b1 = BLOCKS[s % NB]
                pool.wait_ge(c_done, it + 2)
                pool.wait_ge(gate_done, GATE_BANKS + GATES * it + 1)
                pool.tensor_tensor(fc[s % 2][:, 0:n], gate[s % 2][0][:, 0:n], cell[:, W * b0:W * b1],
                                   ALU.mult).then_inc(fc_done, 1)

            def place(j, s):
                b0, b1 = BLOCKS[s % NB]
                pool.wait_ge(ht_done, 2 * NB * j + s + 1)
                pool.wait_ge(par_in, 16)
                pool.tensor_copy(img32[:, b0:b1, 2 * j + s // NB, :],
                                 hT[s % 2][:, 0:width(s % NB)].rearrange("p (b w) -> p b w", w=W)).then_inc(row_done, 1)

            forget(0, 0)
            with pool.Fori(0, H // 2 - 1) as j:
                for s in range(2 * NB):
                    forget(j + (s + 1) // (2 * NB), (s + 1) % (2 * NB))
                    place(j, s)
            for s in range(2 * NB):
                if s < 2 * NB - 1:
                    forget(H // 2 - 1, s + 1)
                place(H // 2 - 1, s)
                if s < CH:
                    pool.wait_ge(xs_in[s], 16)
                    pool.wait_ge(h_upper, s + 1)
                    upper = img32[:, s, 0:H // 2].rearrange("p h w -> p (h w)")
                    pool.tensor_tensor(upper, upper, xs[s][:, 0:HW // 2], ALU.add).then_inc(x1_upper, 1)
            pool.wait_ge(blocks_in, 16 * BLOCK_COPIES)
            pool.wait_ge(row_done, ROW_AHEAD + ITEMS)
            for t in pad:
                pool.memset(flat(t[:]).bitcast(F32), 0.0).then_inc(pads_zero, 1)
            pool.wait_ge(pads_zero, 2)
            def clear_quarter(t, count):
                pool.memset(t[3 * 32:P].rearrange("p q a b -> p (q a b)").bitcast(F32), 0.0).then_inc(pads_zero, 1)
                pool.wait_ge(pads_zero, count)

            clear_quarter(shifted[0], 3)

            def low(b, slot):
                pool.wait_ge(hi_done, b + 1)
                pool.tensor_tensor(interior(pad[slot], 1), xn[slot][:].rearrange("p (h w) -> p h w", w=W),
                                   interior(pad[slot], 0), ALU.subtract).then_inc(lo_done, 1)

            def add_up(b, slot):
                pool.wait_ge(y_done, 2 * b + 2)
                pool.tensor_tensor(ybuf[slot][:], ybuf[slot][:], img32[:, b].rearrange("p h w -> p (h w)"),
                                   ALU.add).then_inc(sum_done, 1)

            low(0, 0)
            pool.wait_ge(lo_done, 1)
            clear_quarter(shifted[1], 4)
            low(1, 1)
            with pool.Fori(1, B // 2) as i:
                for u in range(2):
                    low(2 * i + u, u)
                    add_up(2 * i + u - 2, u)
            add_up(B - 2, 0)

        @block.scalar
        def _(act):
            def turn_weights():
                act.wait_ge(scales_ready, 1)
                for t, raw, k, scale in ((turn_i, raw_i, 2, scl[:, 4:5]), (turn_c, raw_c, 9, scl[:, 5:6])):
                    act.activation(t[:].rearrange("p k (q n) -> p k q n", q=Q),
                                   raw[:].rearrange("p (n q) k -> p k q n", q=Q)[:, 0:k], ACT.Identity,
                                   scale=scale).then_inc(raws_ready, 1)
                act.activation(raw_s[:], raw_s[:], ACT.Identity, scale=scl[:, 4:5]).then_inc(raws_ready, 1)

            def square_root(g):
                act.wait_ge(gn_step, GN_STEPS * g + 5)
                act.activation(sd[:], var_eps[:], ACT.Sqrt, scale=1.0 / ACT_SCALE ** 2).then_inc(sd_done, 1)

            def chunk0(g, last):
                def norm_image(j):
                    act.wait_ge(lo0_done, CH * g + j + 1)
                    act.activation(xn0[j][:], img32[:, CH * g + j].rearrange("p h w -> p (h w)"), ACT.Identity,
                                   bias=nbias[:, j:j + 1], scale=rstd[:, j:j + 1]).then_inc(xn0_done, 1)

                by_dve = 2 if last else 1

                def high_image(j):
                    if j < by_dve:
                        act.wait_ge(xn0v_done, g + j + 1)
                    else:
                        act.wait_ge(xn0_done, (CH - 1) * g + j + 1 - by_dve)
                    act.activation(img[:, CH * g + j, :, 0, :], xn0[j][:].rearrange("p (h w) -> p h w", w=W),
                                   ACT.Copy).then_inc(hi0_done, 1)

                act.wait_ge(gn_step, GN_STEPS * (g + 1))
                for j in range(1, CH):
                    if j >= by_dve:
                        norm_image(j)
                    if j < CH - 1:
                        high_image(j - 1)
                if not last:
                    square_root(g + 1)
                high_image(CH - 2)
                high_image(CH - 1)

            act.wait_ge(warm_set, 1)
            act.activation(warm[:, 2:3], warm[:, 0:1], ACT.Sqrt).then_inc(warmed, 1)
            square_root(0)
            for g in range(2):
                chunk0(g, False)
            turn_weights()
            with act.Fori(2, CHUNKS - 1) as g:
                chunk0(g, False)
            chunk0(CHUNKS - 1, True)
            act.wait_ge(prep_T, 6)
            act.activation(wall_hi[:], wconv_ps, ACT.Copy).then_inc(wall_hi_done, 1)

            def high_z(it, s):
                n = width(s % NB)
                act.wait_ge(z_ready, it + 1)
                act.activation(z_hi[:, 0:n], zbank(s)[:, 0:n], ACT.Identity, scale=z_unscale[:]).then_inc(z_hi_done, 1)

            def item(j, s, last):
                it = 2 * NB * j + s
                n = width(s % NB)
                b0, b1 = BLOCKS[s % NB]
                p = s % 2
                act.wait_ge(h_done, it + 1)
                for m, gt in enumerate(GATE_ORDER):
                    act.wait_ge(gate_ready, GATES * it + m + 1)
                    act.activation(gate[p][m][:, 0:n], gbank(s, m)[:, 0:n],
                                   ACT.Tanh if gt == G_GATE else ACT.Sigmoid,
                                   bias=gate_bias[:, gt:gt + 1]).then_inc(gate_done, 1)
                if not last:
                    high_z(it + 1, s + 1)
                act.wait_ge(c_done, NB + it + 1)
                act.activation(tc[p][:, 0:n], cell[:, W * b0:W * b1], ACT.Tanh).then_inc(tc_done, 1)

            act.activation(warm[:, 1:2], warm[:, 0:1], ACT.Sigmoid).then_inc(warmed, 1)
            high_z(0, 0)
            act.wait_ge(gate_bias_done, 1)
            with act.Fori(0, H // 2 - 1) as j:
                for s in range(2 * NB):
                    item(j, s, False)
            for s in range(2 * NB):
                item(H // 2 - 1, s, s == 2 * NB - 1)
                if s < CH:
                    act.wait_ge(row_done, ROW_AHEAD + NB * H // 2)
                    act.activation(img32[:, s, 0:H // 2], img32[:, s, 0:H // 2], ACT.Copy,
                                   scale=1.0 / ACT_SCALE).then_inc(h_upper, 1)

            def norm(b, j, free):
                if free:
                    act.wait_ge(lo_done, b - 1)
                act.activation(xn[j % 2][:], img32[:, b].rearrange("p h w -> p (h w)"), ACT.Identity,
                               bias=nbias[:, j:j + 1], scale=rstd[:, j:j + 1]).then_inc(xn_done, 1)

            def high(b, j, free):
                if free:
                    act.wait_ge(pads_used, b - 1)
                act.wait_ge(xn_done, b + 1)
                act.activation(interior(pad[j % 2], 0), xn[j % 2][:].rearrange("p (h w) -> p h w", w=W),
                               ACT.Copy).then_inc(hi_done, 1)

            def last_shift(b, j, free):
                act.wait_ge(lo_done, b + 1)
                if free:
                    act.wait_ge(conv_done, 2 * b - 2)
                act.activation(shift_to(j % 2, *SHIFTS[-1]), shift_from(j % 2, *SHIFTS[-1]), ACT.Copy).then_inc(last_shift_done, 1)

            def evacuate(b, j, half_b, s):
                if s == 0:
                    act.wait_ge(stored[j % 2], 16 * half_b)
                act.wait_ge(conv_done, 2 * b + s + 1)
                act.activation(ybuf[j % 2][:, 512 * s:512 * s + 512], ps[:, (2 * j + s) % 4, :], ACT.Identity,
                               bias=conv_bias[:], scale=y_unscale[:]).then_inc(y_done, 1)

            def chunk1(c, first, last):
                for j in range(CH):
                    b = CH * c + j
                    if first and j == 0:
                        act.wait_ge(gn_step, GN_STEPS * (CHUNKS + 1))
                    norm(b, j, not first or j >= 2)
                    high(b, j, not first or j >= 2)
                    if not first or j >= 1:
                        last_shift(b - 1, (j - 1) % CH, not first or j >= 3)
                    if not first or j >= 2:
                        evacuate(b - 2, (j - 2) % CH, 2 * c + (j - 2) // 2, 0)
                    if j == CH - 1 and not last:
                        square_root(CHUNKS + c + 1)
                    if not first or j >= 2:
                        evacuate(b - 2, (j - 2) % CH, 2 * c + (j - 2) // 2, 1)
                    if j == CH - 1 and not last:
                        act.wait_ge(gn_step, GN_STEPS * (CHUNKS + c + 2))

            act.activation(warm[:, 3:4], warm[:, 0:1], ACT.Sqrt).then_inc(warmed, 1)
            square_root(CHUNKS)
            act.wait_ge(pads_zero, 2)
            chunk1(0, True, False)
            with act.Fori(1, CHUNKS - 1) as c:
                chunk1(c, False, False)
            chunk1(CHUNKS - 1, False, True)
            last_shift(B - 1, CH - 1, True)
            for b in range(B - 2, B):
                for s in range(2):
                    evacuate(b, b % CH, B // 2 - 1, s)

        @block.tensor
        def _(pe):
            def sum_means(g):
                pe.wait_ge(aggr_done, CH * (g + 1))
                pe.matmul(gn_ps[:, 0:CH], group_mean[:], mv[:, :, 0], start=True, stop=True).then_inc(mean_ready, 1)

            def sum_vars(g):
                pe.wait_ge(gn_step, GN_STEPS * g + 4)
                pe.matmul(gn_ps[:, CH:2 * CH], group_mean[:], vdev[:], start=True, stop=True).then_inc(var_ready, 1)

            pe.wait_ge(group_in, 16)
            with pe.Fori(0, CHUNKS - 2) as g:
                sum_means(g)
                sum_vars(g)
            pe.wait_ge(raws_ready, 3)
            for k in range(2):
                ins = pe.transpose(wgroup(0)[:, k, :], turn_i[:, k, :], ident[:])
            ins.then_inc(prep_T, 1)
            for k in range(3):
                ins = pe.transpose(wgroup(1)[:, k, :], raw_s[:, :, k], ident[:])
            ins.then_inc(prep_T, 1)
            for k in range(GATES):
                ins = pe.transpose(wgroup(2)[:, k, :], raw_g[:, k, :], ident[:])
            ins.then_inc(prep_T, 1)
            for d in range(3):
                for e in range(3):
                    ins = pe.transpose(wconv_ps[:, d, e, :], turn_c[:, 3 * d + e, :], ident[:])
                ins.then_inc(prep_T, 1)
            for g in range(CHUNKS - 2, CHUNKS):
                sum_means(g)
                sum_vars(g)
            pe.wait_ge(wgt_done, 1)
            pe.wait_ge(bias_ready, 1)
            for k in range(GATES):
                ins = pe.matmul(ps[:, 6, k:k + 1], wgT[:, k, :], bsum[:, 0:1], start=True, stop=True)
            ins.then_inc(prep_T, 1)

            PASSES_I = ((wi_hi, 0), (wi_lo, 0), (wi_hi, 1))

            def input_conv(t, s, k, alone):
                b0, b1 = BLOCKS[k]
                z = zbank(s)[:, 0:width(k)].rearrange("p (b w) -> p b w", w=W)
                for m, (w, half) in enumerate(PASSES_I):
                    pe.matmul(z, w[:, 1, :], img[:, b0:b1, t, half, :], start=(m == 0), stop=False)
                    ins = pe.matmul(z[:, :, 1:W], w[:, 0, :], img[:, b0:b1, t, half, 0:W - 1], start=False,
                                    stop=alone and m == 2)
                if alone:
                    ins.then_inc(z_ready, 1)

            def state_conv(j, s):
                u, k = s // NB, s % NB
                b0, b1 = BLOCKS[k]
                z = zbank(s)[:, 0:width(k)]
                pe.wait_ge(hh_done, NB * (2 * j + u) + min(k + 2, NB))
                for w in (ws_hi, ws_lo):
                    for tap in range(3):
                        pe.matmul(z, w[:, tap, :], hh[1 - u][:, W * b0 + tap:W * b1 + tap], start=False, stop=False)
                pe.wait_ge(hl_done, NB * (2 * j + u) + min(k + 2, NB))
                for tap in range(3):
                    ins = pe.matmul(z, ws_hi[:, tap, :], hl[1 - u][:, W * b0 + tap:W * b1 + tap],
                                    start=False, stop=(tap == 2))
                ins.then_inc(z_ready, 1)

            def item(j, s, zero_state, last):
                k = s % NB
                it = 2 * NB * j + s
                n = width(k)
                if not (zero_state and s < NB):
                    state_conv(j, s)
                if not last:
                    pe.wait_ge(z_lo_done, it + 1)
                    input_conv(2 * j + (s + 1) // NB, s + 1, (k + 1) % NB, zero_state and s + 1 < NB)
                pe.wait_ge(z_hi_done, it + 1)
                for m in range(2):
                    pe.wait_ge(gate_done, GATES * it + m + 1)
                    pe.matmul(gbank(s, m)[:, 0:n], wg_hi[:, GATE_ORDER[m], :], z_hi[:, 0:n], start=True, stop=False)
                    pe.matmul(gbank(s, m)[:, 0:n], wg_lo[:, GATE_ORDER[m], :], z_hi[:, 0:n], start=False, stop=False)
                pe.wait_ge(z_lo_done, Z_AHEAD + it + 1)
                for m in range(2):
                    pe.matmul(gbank(s, m)[:, 0:n], wg_hi[:, GATE_ORDER[m], :], z_lo[:, 0:n],
                              start=False, stop=True).then_inc(gate_ready, 1)
                for m in range(2, GATES):
                    pe.wait_ge(gate_done, GATES * it + m + 1)
                    pe.matmul(gbank(s, m)[:, 0:n], wg_hi[:, GATE_ORDER[m], :], z_hi[:, 0:n], start=True, stop=False)
                    pe.matmul(gbank(s, m)[:, 0:n], wg_lo[:, GATE_ORDER[m], :], z_hi[:, 0:n], start=False, stop=False)
                    pe.matmul(gbank(s, m)[:, 0:n], wg_hi[:, GATE_ORDER[m], :], z_lo[:, 0:n],
                              start=False, stop=True).then_inc(gate_ready, 1)

            pe.wait_ge(lo0_done, LO0_DONE)
            pe.wait_ge(lo0v_done, CH // 2)
            pe.wait_ge(split_done, 1)
            input_conv(0, 0, 0, True)
            pe.wait_ge(split_done, 4)
            pe.wait_ge(gate_bias_done, 1)
            for s in range(2 * NB):
                item(0, s, True, False)
            with pe.Fori(1, H // 2 - 1) as j:
                for s in range(2 * NB):
                    item(j, s, False, False)
            for s in range(2 * NB):
                item(H // 2 - 1, s, False, s == 2 * NB - 1)

            DENSE = ((wc_hi, 0), (wc_lo, 0), (wc_hi, 1))
            TILED = ((wt_hi, 0), (wt_lo, 0), (wt_hi, 1))

            def bank(j, s):
                return ps[:, (2 * j + s) % 4, :].rearrange("p (h w) -> p h w", w=W)

            def dense_half(b, j, s, free):
                if free:
                    pe.wait_ge(y_done, 2 * b + s - 3)
                for m, (w, part) in enumerate(DENSE):
                    pe.matmul(bank(j, s), w[:], padded(pad[j % 2][:, part, :], s, 0, 0), start=(m == 0), stop=False,
                              skip_group_check=True)

            def tiled_half(j, s):
                for m, (w, part) in enumerate(TILED):
                    for d in range(3):
                        for q in range(Q):
                            ins = pe.matmul(bank(j, s)[32 * q:32 * q + 32], w[:, d, q, :],
                                            padded(shifted[j % 2][:, q, part, :], s, d - 1, 0), start=False,
                                            stop=(m == 2 and d == 2), tile_position=(0, 32 * q), skip_group_check=True)
                            if m == d == q == s == 0:
                                ins.then_inc(pads_used, 1)
                ins.then_inc(conv_done, 1)

            def chunk1(c, first, last):
                for j in range(CH):
                    b = CH * c + j
                    pe.wait_ge(lo_done, b + 1)
                    dense_half(b, j, 0, not first or j >= 2)
                    dense_half(b, j, 1, not first or j >= 2)
                    pe.wait_ge(shifted_in[j % 2], 16 * (len(SHIFTS) - 1) * (2 * c + j // 2 + 1))
                    pe.wait_ge(last_shift_done, b + 1)
                    pe.wait_ge(unshifted_done, Q * (b + 1))
                    tiled_half(j, 0)
                    if j == 1 and not last:
                        sum_means(CHUNKS + c + 1)
                    tiled_half(j, 1)
                    if j == 1 and not last:
                        sum_vars(CHUNKS + c + 1)

            pe.wait_ge(blocks_in, 16 * BLOCK_COPIES)
            pe.wait_ge(gate_done, GATE_BANKS + GATES * ITEMS)
            sum_means(CHUNKS)
            sum_vars(CHUNKS)
            pe.wait_ge(pads_zero, 3)
            chunk1(0, True, False)
            with pe.Fori(1, CHUNKS - 1) as c:
                chunk1(c, False, False)
            chunk1(CHUNKS - 1, False, True)


_INS = ["x", "L0_conv_w_i2s", "L0_conv_b_i2s", "L0_conv_w_s2s", "L0_conv_b_s2s", "L0_conv_w_ih", "L0_conv_b_ih",
        "L0_conv_b_hh", "L1_conv_W", "L1_conv_b"]


def shape_constants():
    c = np.arange(P)
    same_group = (c[:, None] % 32 == c[None, :] % 32).astype(np.float32) / Q
    kept = (c[:, None] % 3 >= c[None, :] % 3).astype(np.float32)
    return np.stack([np.eye(P, dtype=np.float32), same_group, kept])


def kernel(**inputs):
    import concourse.bacc as _bacc
    from concourse.bass_utils import run_bass_kernel_spmd as _run

    nc = _bacc.Bacc("TRN2", target_bir_lowering=False, num_devices=1)
    arrays, args = {}, []
    for name in _INS:
        a = np.ascontiguousarray(inputs[name])
        arrays[f"in_{name}_dram"] = a
        args.append(nc.dram_tensor(f"in_{name}_dram", a.shape, mybir.dt.from_np(a.dtype), kind="ExternalInput").ap())
    arrays["in_consts_dram"] = shape_constants()
    args.append(nc.dram_tensor("in_consts_dram", (3, P, P), F32, kind="ExternalInput").ap())
    out = nc.dram_tensor("out_0_dram", (B, P, H, W), F32, kind="ExternalOutput").ap()
    build_network(nc, *args, out)
    r = _run(nc, [arrays], core_ids=[0])
    return r.results[0]["out_0_dram"]
```
